# Optimizing a Trainium2 kernel written in Bass

```python
import numpy as np
import jax
import jax.numpy as jnp

def _softmax(x, axis=-1):
    return jax.nn.softmax(x, axis=axis)

def _gelu(x):
    return jax.nn.gelu(x, approximate=True)

def _silu(x):
    return jax.nn.silu(x)

def _sigmoid(x):
    return jax.nn.sigmoid(x)

def _layernorm(x, axis=-1, eps=1e-05):
    m = jnp.mean(x, axis=axis, keepdims=True)
    v = jnp.var(x, axis=axis, keepdims=True)
    return (x - m) / jnp.sqrt(v + eps)

def _scatter_add(tgt, idx, src, axis=0):
    return tgt.at[idx].add(src)

def _segment_sum(src, seg, n):
    return jax.ops.segment_sum(src, seg, n)
kernel_name = 'mk_adj_resnorm_d1_adj_r2_2c1de7'

def setup_inputs(seed: int=0):
    np.random.seed(seed)
    _w = jnp.asarray

    def _rec_inputs():
        import jax
        import jax.numpy as jnp
        _gk = jax.random.key(seed)
        x = -0.000929 + 1 * jax.random.normal(jax.random.fold_in(_gk, 1), (8192, 128), jnp.float32)
        _a = jax.random.bernoulli(jax.random.fold_in(_gk, 2), 0.000244141, (8192, 8192))
        _a = jnp.logical_or(_a, jnp.eye(8192, dtype=bool))
        _af = _a.astype(jnp.float32)
        _af = _af * jax.random.uniform(jax.random.fold_in(_gk, 3), (8192, 8192), jnp.float32, 0.05, 1)
        adj = _af
        return (x, adj)
    x, adj = _rec_inputs()

    def _L0_gnn_setup():
        import jax, jax.numpy as jnp
        import numpy as np
        N = 4096
        F_IN = 128
        F_OUT = 128
        key = jax.random.key(seed)
        k1, k2, k3, k4 = jax.random.split(key, 4)
        x = jax.random.normal(k1, (N, F_IN), dtype=jnp.float32)
        adjacency = jax.random.uniform(k2, (N, N), dtype=jnp.float32)
        W = jax.random.normal(k3, (F_OUT, F_IN), dtype=jnp.float32) * (1.0 / np.sqrt(F_IN))
        b = jax.random.normal(k4, (F_OUT,), dtype=jnp.float32) * 0.01
        return {'x': x, 'adjacency': adjacency, 'W': W, 'b': b}
    _L0_gnn_all = _L0_gnn_setup()
    _L0_gnn_in = {k: v for k, v in _L0_gnn_all.items() if k in ('W', 'b')}
    del _L0_gnn_all
    return {'x': x, 'adj': adj, 'L0_gnn_W': _L0_gnn_in['W'], 'L0_gnn_b': _L0_gnn_in['b']}

def reference(x, adj, L0_gnn_W, L0_gnn_b):
    import jax
    import jax.numpy as jnp

    def _L0_gnn_ref(x, adjacency, W, b):
        import jax, jax.numpy as jnp
        import numpy as np
        N = 4096
        F_IN = 128
        F_OUT = 128
        a_hat = adjacency + jnp.eye(adjacency.shape[0], dtype=adjacency.dtype)
        dinv = jnp.sum(a_hat, axis=1) ** (-0.5)
        a_norm = dinv[:, None] * a_hat * dinv[None, :]
        support = x @ W.T + b
        return a_norm @ support
    x = _layernorm(x + _L0_gnn_ref(x, adj, L0_gnn_W, L0_gnn_b), axis=-1)
    return x

_drawn_inputs = setup_inputs


def setup_inputs(seed=0):
    import zlib

    import numpy as np

    out = dict(_drawn_inputs(seed))
    spreads = {}
    factors = {'L0_gnn_b': 6.437}
    for name, (base, spread) in spreads.items():
        noise = np.random.default_rng([zlib.crc32(name.encode()), seed]).standard_normal(out[name].shape)
        drawn = base * np.exp(spread * noise) if base else spread * noise
        out[name] = jnp.asarray(drawn.astype(out[name].dtype))
    for name, factor in factors.items():
        out[name] = (out[name] * factor).astype(out[name].dtype)
    return out
```

```python
from contextlib import ExitStack

import concourse.bass as bass
from concourse import mybir

F32 = mybir.dt.float32
ALU = mybir.AluOpType
ACT = mybir.ActivationFunctionType
AX_X = mybir.AxisListType.X

P = 128
T = 4
CH = T * P
U = 4
RING = U
RRING = U
FIN = 4
EPS = 1e-5


def runs(first, end):
    trips = max(end - first, 0) // U
    looped = trips if trips > 1 else 0
    return ([(first, looped)] if looped else []) + [(k, 0) for k in range(first + looped * U, end)]


def each(eng, spans, body):
    for base, trips in spans:
        if trips:
            with eng.Fori(0, trips) as q:
                for i in range(base, base + U):
                    body(i, q)
        else:
            body(base, 0)


def resnorm_gnn(nc, x, adj, W, b, out):
    N, F = x.shape
    G = N // CH
    assert F == P and tuple(adj.shape) == (N, N) and N % CH == 0 and G > 2 * U
    LAST = G - 1

    def unit_row(g):
        return g * g

    def unit_d(g):
        return g * g + g

    def unit_c(g):
        return g * g + g + 1

    def l_before(g):
        return g * (g - 1) // 2

    def summed_before(g):
        return g * (g + 1) // 2

    def r_count(g):
        return G - 1 - g

    def r_before(g):
        return sum(r_count(h) for h in range(g))

    x_g = x.rearrange("(g t p) f -> g p t f", p=P, t=T)
    out_g = out.rearrange("(g t p) f -> g p t f", p=P, t=T)

    def group(ap, g):
        return ap[g] if isinstance(g, int) else ap[bass.ds(g, 1)].rearrange("a p t f -> (a p) t f")

    def chunk(g, c):
        return adj[bass.ds(g * CH, CH), bass.ds(c * CH, CH)].rearrange("(t p) c -> p t c", p=P)

    with ExitStack() as ctx:
        def sb(name, shape):
            return ctx.enter_context(nc.sbuf_tensor(name, shape, F32))

        def sem(name):
            return ctx.enter_context(nc.semaphore(name))

        def bank(name, n):
            return ctx.enter_context(nc.psum_tensor(name, [P, n, CH], F32))

        ring = sb("ring", [P, RING, T, CH])
        r_ring = sb("r_ring", [P, RRING, T, CH])
        support = sb("support", [P, G, T, F])
        y_acc = sb("y_acc", [P, G, CH])
        a_t = sb("a_t", [P, T, CH])
        l_stage = sb("l_stage", [P, 2, T, F])
        d_stage = sb("d_stage", [P, 2, T, F])
        part = sb("part", [P, 2, T, G])
        row_sum = sb("row_sum", [P, 2, T])
        deg = sb("deg", [P, G, T])
        dinv = sb("dinv", [P, G, T])
        neg_half = sb("neg_half", [P, T])
        ident = sb("ident", [P, P])
        w_rows = sb("w_rows", [P, F])
        w_t = sb("w_t", [P, F])
        ones = sb("ones", [1, P])
        bias = sb("bias", [1, F])
        x_rows = sb("x_rows", [P, 2, T, F])
        x_t = sb("x_t", [P, 2, CH])
        y_last = sb("y_last", [P, 2, CH])
        x_res = sb("x_res", [P, FIN, T, F])
        z = sb("z", [P, FIN, T, F])
        stats = sb("stats", [P, T, 6])
        halves = sb("halves", [P, FIN, 3, T])
        diff_sq = sb("diff_sq", [P, T])
        diff_var = sb("diff_var", [P, T])
        half_var = sb("half_var", [P, T])
        var_eps = sb("var_eps", [P, T])
        neg_mean = sb("neg_mean", [P, T])
        rstd = sb("rstd", [P, FIN, T])
        shift = sb("shift", [P, FIN, T])
        y_out = sb("y_out", [P, 2, T, F])

        ps_t = bank("ps_t", T)
        ps_row = bank("ps_row", 1)
        ps_col = bank("ps_col", 2)
        ps_fin = bank("ps_fin", 1)

        const_in = sem("const_in")
        x_in = [sem(f"x_in{k}") for k in range(2)]
        ring_in = [sem(f"ring_in{k}") for k in range(RING)]
        r_in = [sem(f"r_in{k}") for k in range(RRING)]
        res_in = [sem(f"res_in{k}") for k in range(FIN)]
        stored = [sem(f"stored{k}") for k in range(2)]
        zeroed = sem("zeroed")
        const_set = sem("const_set")
        wt_done = sem("wt_done")
        wt_copied = sem("wt_copied")
        xt_done = sem("xt_done")
        xt_copied = sem("xt_copied")
        sup_done = sem("sup_done")
        sup_copied = sem("sup_copied")
        trans_done = sem("trans_done")
        evac_done = sem("evac_done")
        mm_done = sem("mm_done")
        ld_summed = sem("ld_summed")
        r_summed = sem("r_summed")
        row_summed = sem("row_summed")
        deg_ready = sem("deg_ready")
        dinv_ready = sem("dinv_ready")
        ds_ready = sem("ds_ready")
        ds_saved = sem("ds_saved")
        l_staged = sem("l_staged")
        row_saved = sem("row_saved")
        col_added = sem("col_added")
        y_turned = sem("y_turned")
        fin_step = sem("fin_step")
        stats_ready = sem("stats_ready")
        pool_step = sem("pool_step")
        scale_ready = sem("scale_ready")
        normed = sem("normed")

        block = ctx.enter_context(nc.Block())

        def ring_at(s0, i):
            return (s0 + i) % RING

        def ring_landed(eng, s0, i, q):
            eng.wait_ge(ring_in[ring_at(s0, i)], (q + ((s0 + i) // RING + 1)) * 16)

        def r_landed(eng, n0, i, q):
            eng.wait_ge(r_in[(n0 + i) % RRING], (q + ((n0 + i) // RRING + 1)) * 16)

        @block.sync
        def _(sp):
            def load_ring(g, c, s0, i, q, summed):
                if not isinstance(summed, int) or summed > 0:
                    sp.wait_ge(ld_summed, summed)
                if s0 + i >= RING:
                    sp.wait_ge(trans_done, (q * U + (s0 + i - RING + 1)) * T)
                slot = ring_at(s0, i)
                sp.dma_start(ring[:, slot], chunk(g, c)).then_inc(ring_in[slot], 16)

            def load_ld(g):
                def body(i, q):
                    n = summed_before(g) + (i - RING + 1 if i >= RING else 0)
                    need = q * U + n if i >= RING else n
                    load_ring(g, q * U + i, unit_row(g), i, q, need)
                return body

            def load_c(g):
                def body(i, q):
                    load_ring(q * U + i, g, unit_c(g), i, q, summed_before(g) + min(max(g + 2 + i - RING, 0), g + 1))
                return body

            def load_r(g):
                def body(i, q):
                    n0 = r_before(g)
                    if n0 + i >= RRING:
                        sp.wait_ge(r_summed, q * U + (n0 + i - RRING + 1))
                    slot = (n0 + i) % RRING
                    sp.dma_start(r_ring[:, slot], chunk(g, q * U + (i + g + 1))).then_inc(r_in[slot], 16)
                return body

            sp.dma_start(w_rows[:], W).then_inc(const_in, 16)
            sp.dma_start(bias[:], b.rearrange("(a f) -> a f", a=1)).then_inc(const_in, 16)
            load_ld(0)(0, 0)
            each(sp, [(k, 0) for k in range(RRING)] + runs(RRING, r_count(0)), load_r(0))
            for g in range(G):
                if g > 0:
                    each(sp, [(k, 0) for k in range(1, min(g, RING))] + runs(RING, g), load_ld(g))
                    load_ld(g)(g, 0)
                both = min(g, r_count(g + 1)) if g < LAST else 0
                peeled = min(g, RING)
                each(sp, [(k, 0) for k in range(min(both, RING))] + runs(RING, both),
                     lambda i, q: (load_c(g)(i, q), load_r(g + 1)(i, q)))
                each(sp, [(k, 0) for k in range(both, peeled)] + runs(max(both, peeled), g), load_c(g))
                if g < LAST:
                    load_ld(g + 1)(0, 0)
                    each(sp, runs(both, r_count(g + 1)), load_r(g + 1))

        @block.gpsimd
        def _(pool):
            nc.gpsimd.memset(ident[:], 0.0).then_inc(zeroed, 1)
            nc.gpsimd.memset(ones[:], 1.0).then_inc(const_set, 1)
            nc.gpsimd.memset(neg_half[:], -0.5).then_inc(const_set, 1)
            pool.wait_ge(zeroed, 1)
            nc.gpsimd.affine_select(out=ident[:], in_=ident[:], compare_op=ALU.not_equal, fill=1.0, base=0,
                                    pattern=[[-1, P]], channel_multiplier=1).then_inc(const_set, 1)
            pool.wait_ge(const_set, 3)

            for g in range(G):
                def stage(i, q):
                    if i < 2:
                        if g > 1:
                            pool.wait_ge(mm_done, unit_d(g - 1) * T)
                        pool.wait_ge(ds_saved, g)
                    else:
                        pool.wait_ge(mm_done, (q * U + (unit_row(g) + i - 1)) * T)
                    nc.gpsimd.tensor_copy(l_stage[:, (l_before(g) + i) % 2],
                                          support[:, bass.ds(q * U + i, 1)].rearrange("p a t f -> p (a t) f"))\
                      .then_inc(l_staged, 1)

                each(pool, [(k, 0) for k in range(min(g, 2))] + runs(2, g), stage)
                pool.wait_ge(deg_ready, g + 1)
                nc.gpsimd.tensor_tensor(dinv[:, g], deg[:, g], neg_half[:], ALU.pow).then_inc(dinv_ready, 1)
                pool.wait_ge(ds_ready, g + 1)
                nc.gpsimd.tensor_copy(support[:, g], d_stage[:, g % 2]).then_inc(ds_saved, 1)

            for e in range(G):
                slot = e % FIN
                pool.wait_ge(stats_ready, e + 1)
                if e >= FIN:
                    pool.wait_ge(normed, e - FIN + 1)
                if e >= 1:
                    pool.wait_ge(scale_ready, e)
                nc.gpsimd.tensor_scalar(neg_mean[:], halves[:, slot, 0], -0.5, None, ALU.mult).then_inc(pool_step, 1)
                nc.gpsimd.tensor_scalar(half_var[:], halves[:, slot, 2], 1.0 / F, EPS, ALU.mult, ALU.add)\
                  .then_inc(pool_step, 1)
                nc.gpsimd.tensor_tensor(diff_sq[:], halves[:, slot, 1], halves[:, slot, 1], ALU.mult)\
                  .then_inc(pool_step, 1)
                pool.wait_ge(pool_step, 6 * e + 3)
                nc.gpsimd.tensor_scalar(diff_var[:], diff_sq[:], 0.25, None, ALU.mult).then_inc(pool_step, 1)
                pool.wait_ge(pool_step, 6 * e + 4)
                nc.gpsimd.tensor_tensor(var_eps[:], diff_var[:], half_var[:], ALU.add).then_inc(pool_step, 1)
                pool.wait_ge(pool_step, 6 * e + 5)
                nc.gpsimd.tensor_tensor(rstd[:, slot], var_eps[:], neg_half[:], ALU.pow).then_inc(pool_step, 1)
                pool.wait_ge(pool_step, 6 * e + 6)
                nc.gpsimd.tensor_tensor(shift[:, slot], neg_mean[:], rstd[:, slot], ALU.mult).then_inc(scale_ready, 1)

        @block.scalar
        def _(act):
            def load_x(i, q, slot):
                act.dma_start(x_rows[:, slot], group(x_g, q * U + i)).then_inc(x_in[slot], 16)

            load_x(0, 0, 0)
            load_x(1, 0, 1)
            act.wait_ge(wt_done, 1)
            nc.scalar.copy(w_t[:], ps_fin[:, 0, 0:F]).then_inc(wt_copied, 1)

            def copy_support(i, q, more):
                slot = i % 2
                act.wait_ge(xt_done, q * U + i + 1)
                if i >= 2:
                    act.wait_ge(sup_done, q * U + (i - 1))
                nc.scalar.copy(x_t[:, slot], ps_t[:, slot]).then_inc(xt_copied, 1)
                if more:
                    load_x(i + 2, q, slot)
                act.wait_ge(sup_done, q * U + i + 1)
                nc.scalar.copy(support[:, bass.ds(q * U + i, 1)].rearrange("p a t f -> p (a t f)"),
                               ps_t[:, 2 + slot]).then_inc(sup_copied, 1)

            each(act, [(0, 0), (1, 0)] + runs(2, G - 2), lambda i, q: copy_support(i, q, True))
            copy_support(G - 2, 0, False)
            copy_support(G - 1, 0, False)

            def evac(s0, i, q, j):
                act.wait_ge(trans_done, (q * U + (s0 + i)) * T + (j + 1))
                if s0 + i >= 1:
                    act.wait_ge(mm_done, (q * U + (s0 + i - 1)) * T + (j + 1))
                nc.scalar.copy(a_t[:, j], ps_t[:, j]).then_inc(evac_done, 1)

            def unit(s0, i, q, more=True):
                evac(s0, i, q, 2)
                evac(s0, i, q, 3)
                if more:
                    evac(s0, i + 1, q, 0)
                    evac(s0, i + 1, q, 1)

            evac(0, 0, 0, 0)
            evac(0, 0, 0, 1)
            for g in range(G):
                each(act, runs(0, g), lambda i, q: unit(unit_row(g), i, q))
                unit(unit_d(g), 0, 0)
                act.wait_ge(mm_done, (unit_d(g) + 1) * T)
                nc.scalar.copy(y_acc[:, g] if g < LAST else y_last[:, 0], ps_row[:, 0]).then_inc(row_saved, 1)
                if g < LAST:
                    each(act, runs(0, g), lambda i, q: unit(unit_c(g), i, q))

            def fin_row(i, q):
                return LAST if (isinstance(q, int) and i == 0) else q * U + (i - 1)

            def load_res(i, q):
                slot = i % FIN
                act.dma_start(x_res[:, slot], group(x_g, fin_row(i, q))).then_inc(res_in[slot], 16)

            def norm(i, q, more):
                slot = i % FIN
                act.wait_ge(scale_ready, q * U + i + 1)
                if i >= 2:
                    act.wait_ge(stored[i % 2], (q * (U // 2) + (i - 2) // 2 + 1) * 16)
                for t in range(T):
                    done = nc.scalar.activation(y_out[:, i % 2, t], z[:, slot, t], ACT.Identity,
                                                bias=shift[:, slot, t:t + 1], scale=rstd[:, slot, t:t + 1])
                done.then_inc(normed, 1)
                if more:
                    load_res(i + FIN, q)
                act.wait_ge(normed, q * U + i + 1)
                act.dma_start(group(out_g, fin_row(i, q)), y_out[:, i % 2]).then_inc(stored[i % 2], 16)

            for e in range(FIN):
                load_res(e, 0)
            s0 = unit_c(LAST)
            for k in range(4):
                unit(s0, k, 0)
                if k >= 2:
                    norm(k - 2, 0, True)
            each(act, runs(4, LAST - 3),
                 lambda i, q: (unit(s0, i, q), norm(i - 2, q, True)))
            for k in range(LAST - 3, LAST):
                unit(s0, k, 0, k < LAST - 1)
                norm(k - 2, 0, k - 2 + FIN < G)
            for e in range(LAST - 2, G):
                norm(e, 0, False)
            act.wait_ge(stored[0], G // 2 * 16)
            act.wait_ge(stored[1], G // 2 * 16)

        @block.vector
        def _(dve):
            def sum_ld(g):
                def body(i, q):
                    ring_landed(dve, unit_row(g), i, q)
                    nc.vector.tensor_reduce(part[:, g % 2, :, bass.ds(q * U + i, 1)].rearrange("p t a -> p (t a)"),
                                            ring[:, ring_at(unit_row(g), i)], AX_X, ALU.add).then_inc(ld_summed, 1)
                return body

            def sum_r(g):
                def body(i, q):
                    n0 = r_before(g)
                    r_landed(dve, n0, i, q)
                    nc.vector.tensor_reduce(
                        part[:, g % 2, :, bass.ds(q * U + (i + g + 1), 1)].rearrange("p t a -> p (t a)"),
                        r_ring[:, (n0 + i) % RRING], AX_X, ALU.add).then_inc(r_summed, 1)
                return body

            def add_c(g):
                def body(i, q):
                    n = l_before(g) + i
                    dve.wait_ge(mm_done, (q * U + (unit_c(g) + i + 1)) * T)
                    rows = y_acc[:, bass.ds(q * U + i, 1)].rearrange("p a c -> p (a c)")
                    to = rows if g < LAST else y_last[:, (i + 1) % 2]
                    nc.vector.tensor_tensor(to, rows, ps_col[:, n % 2], ALU.add).then_inc(col_added, 1)
                return body

            each(dve, runs(0, r_count(0)), sum_r(0))
            for g in range(G):
                each(dve, runs(0, g), sum_ld(g))
                sum_ld(g)(g, 0)
                dve.wait_ge(ld_summed, summed_before(g + 1))
                dve.wait_ge(r_summed, r_before(g + 1))
                nc.vector.tensor_reduce(row_sum[:, g % 2], part[:, g % 2], AX_X, ALU.add).then_inc(row_summed, 1)
                dve.wait_ge(row_summed, g + 1)
                nc.vector.tensor_scalar(deg[:, g], row_sum[:, g % 2], 1.0, None, ALU.add).then_inc(deg_ready, 1)
                dve.wait_ge(sup_copied, G)
                if g >= 2:
                    dve.wait_ge(mm_done, unit_row(g - 1) * T)
                    dve.wait_ge(ds_saved, g - 1)
                dve.wait_ge(dinv_ready, g + 1)
                nc.vector.tensor_tensor(d_stage[:, g % 2], support[:, g],
                                        dinv[:, g].unsqueeze(2).to_broadcast([P, T, F]), ALU.mult)\
                  .then_inc(ds_ready, 1)
                if g < LAST:
                    if g > 0:
                        dve.wait_ge(row_saved, g)
                        dve.wait_ge(col_added, l_before(g))
                    both = min(g, r_count(g + 1))
                    each(dve, runs(0, both), lambda i, q: (add_c(g)(i, q), sum_r(g + 1)(i, q)))
                    each(dve, runs(both, g), add_c(g))
                    each(dve, runs(both, r_count(g + 1)), sum_r(g + 1))

            def finish(i, q):
                slot = i % FIN
                row = LAST if (isinstance(q, int) and i == 0) else q * U + (i - 1)
                e = q * U + i
                if i >= FIN:
                    dve.wait_ge(normed, e - (FIN - 1))
                dve.wait_ge(y_turned, e + 1)
                if isinstance(row, int):
                    ds, d = support[:, row], dinv[:, row]
                else:
                    ds = support[:, bass.ds(row, 1)].rearrange("p a t f -> p (a t) f")
                    d = dinv[:, bass.ds(row, 1)].rearrange("p a t -> p (a t)")
                turned = ps_fin[:, 0].rearrange("p (t f) -> p t f", f=F)
                nc.vector.tensor_tensor(z[:, slot], turned, ds, ALU.add).then_inc(fin_step, 1)
                dve.wait_ge(fin_step, e * 4 + 1)
                nc.vector.tensor_tensor(z[:, slot], z[:, slot], d.unsqueeze(2).to_broadcast([P, T, F]), ALU.mult)\
                  .then_inc(fin_step, 1)
                dve.wait_ge(fin_step, e * 4 + 2)
                dve.wait_ge(res_in[slot], (q + i // FIN + 1) * 16)
                nc.vector.tensor_tensor(z[:, slot], z[:, slot], x_res[:, slot], ALU.add).then_inc(fin_step, 1)
                dve.wait_ge(fin_step, e * 4 + 3)
                for t in range(T):
                    done = nc.vector.bn_stats(stats[:, t], z[:, slot, t])
                done.then_inc(fin_step, 1)
                dve.wait_ge(fin_step, e * 4 + 4)
                mean_e, mean_o = stats[:, :, 1], stats[:, :, 4]
                nc.vector.tensor_tensor(halves[:, slot, 0], mean_e, mean_o, ALU.add)
                nc.vector.tensor_tensor(halves[:, slot, 1], mean_e, mean_o, ALU.subtract)
                nc.vector.tensor_tensor(halves[:, slot, 2], stats[:, :, 2], stats[:, :, 5], ALU.add)\
                  .then_inc(stats_ready, 1)

            dve.wait_ge(row_saved, LAST)
            dve.wait_ge(ds_saved, G)
            dve.wait_ge(col_added, l_before(LAST))

            def last(i, q):
                if i >= 2:
                    dve.wait_ge(y_turned, q * U + i)
                add_c(LAST)(i, q)
                finish(i, q)

            each(dve, [(k, 0) for k in range(4)] + runs(4, LAST), last)
            finish(LAST, 0)

        @block.tensor
        def _(pe):
            pe.wait_ge(const_in, 32)
            pe.wait_ge(const_set, 3)
            nc.tensor.transpose(ps_fin[:, 0, 0:F], w_rows[:], ident[:]).then_inc(wt_done, 1)

            def turn_x(i, q):
                slot = i % 2
                pe.wait_ge(x_in[slot], (q * (U // 2) + (i // 2 + 1)) * 16)
                if i >= 2:
                    pe.wait_ge(xt_copied, q * U + (i - 1))
                for t in range(T):
                    done = nc.tensor.transpose(ps_t[:, slot, t * P:(t + 1) * P], x_rows[:, slot, t], ident[:])
                done.then_inc(xt_done, 1)

            def mul_x(i, q):
                slot = i % 2
                pe.wait_ge(xt_copied, q * U + i + 1)
                if i >= 2:
                    pe.wait_ge(sup_copied, q * U + (i - 1))
                for t in range(T):
                    to = ps_t[:, 2 + slot, t * F:(t + 1) * F]
                    nc.tensor.matmul(to, x_t[:, slot, t * P:(t + 1) * P], w_t[:], start=True, stop=False)
                    done = nc.tensor.matmul(to, ones[:], bias[:], start=False, stop=True)
                done.then_inc(sup_done, 1)

            turn_x(0, 0)
            pe.wait_ge(wt_copied, 1)
            each(pe, [(0, 0)] + [(k, 0) for k in range(1, 3)] + runs(3, G - 1),
                 lambda i, q: (turn_x(i + 1, q), mul_x(i, q)))
            mul_x(G - 1, 0)
            pe.wait_ge(sup_copied, G)

            def turn(s0, i, q, j):
                if j == 0:
                    ring_landed(pe, s0, i, q)
                slot = ring_at(s0, i)
                for t in range(T):
                    done = nc.tensor.transpose(ps_t[:, j, t * P:(t + 1) * P],
                                               ring[:, slot, t, j * P:(j + 1) * P], ident[:])
                done.then_inc(trans_done, 1)

            def mul(s0, i, q, j, weights, to, start, stop):
                pe.wait_ge(evac_done, (q * U + (s0 + i)) * T + (j + 1))
                nc.tensor.matmul(to, weights[:, j], a_t[:, j], start=start, stop=stop).then_inc(mm_done, 1)

            def unit(s0, i, q, weights, to, opens, closes, more=True):
                turn(s0, i, q, 2)
                mul(s0, i, q, 0, weights, to, opens, False)
                turn(s0, i, q, 3)
                mul(s0, i, q, 1, weights, to, False, False)
                if more:
                    turn(s0, i + 1, q, 0)
                mul(s0, i, q, 2, weights, to, False, False)
                if more:
                    turn(s0, i + 1, q, 1)
                mul(s0, i, q, 3, weights, to, False, closes)

            def unit_of_l(g):
                def body(i, q):
                    n = l_before(g) + i
                    pe.wait_ge(l_staged, q * U + (n + 1))
                    if i == 0:
                        pe.wait_ge(row_saved, g)
                    unit(unit_row(g), i, q, l_stage[:, n % 2], ps_row[:, 0], i == 0, False)
                return body

            def unit_of_c(g, more=True):
                def body(i, q):
                    n = l_before(g) + i
                    if n >= 2:
                        pe.wait_ge(col_added, q * U + (n - 1))
                    unit(unit_c(g), i, q, d_stage[:, g % 2], ps_col[:, n % 2], True, True, more)
                return body

            turn(0, 0, 0, 0)
            turn(0, 0, 0, 1)
            for g in range(G):
                if g > 0:
                    each(pe, [(0, 0)] + runs(1, g), unit_of_l(g))
                pe.wait_ge(ds_ready, g + 1)
                unit(unit_d(g), 0, 0, d_stage[:, g % 2], ps_row[:, 0], g == 0, True)
                if g < LAST:
                    each(pe, runs(0, g), unit_of_c(g))

            def turn_back(i, q):
                e = q * U + i
                if i == 0:
                    pe.wait_ge(row_saved, G)
                else:
                    pe.wait_ge(col_added, e + l_before(LAST))
                    pe.wait_ge(fin_step, e * 4 - 3)
                for t in range(T):
                    done = nc.tensor.transpose(ps_fin[:, 0, t * P:(t + 1) * P],
                                               y_last[:, i % 2, t * P:(t + 1) * P], ident[:])
                done.then_inc(y_turned, 1)

            each(pe, [(0, 0)] + runs(1, LAST - 1), lambda i, q: (unit_of_c(LAST)(i, q), turn_back(i, q)))
            unit_of_c(LAST, False)(LAST - 1, 0)
            turn_back(LAST - 1, 0)
            turn_back(LAST, 0)


_INS = ['x', 'adj', 'L0_gnn_W', 'L0_gnn_b']


def kernel(**inputs):
    import numpy as _np
    import concourse.bacc as _bacc
    from concourse import mybir as _mybir
    from concourse.bass_utils import run_bass_kernel_spmd as _run

    nc = _bacc.Bacc("TRN2", target_bir_lowering=False, num_devices=1)
    arrays, args = {}, []
    for name in _INS:
        a = _np.ascontiguousarray(inputs[name])
        arrays[f"in_{name}_dram"] = a
        args.append(nc.dram_tensor(f"in_{name}_dram", a.shape, _mybir.dt.from_np(a.dtype), kind="ExternalInput").ap())
    x = arrays["in_x_dram"]
    args.append(nc.dram_tensor("out_0_dram", x.shape, _mybir.dt.from_np(x.dtype), kind="ExternalOutput").ap())
    resnorm_gnn(nc, *args)
    r = _run(nc, [arrays], core_ids=[0])
    return r.results[0]["out_0_dram"]
```

```python
from contextlib import ExitStack

import concourse.bass as bass
from concourse import mybir

F32 = mybir.dt.float32
F32R = mybir.dt.float32r
BF16 = mybir.dt.bfloat16
ALU = mybir.AluOpType
ACT = mybir.ActivationFunctionType
AX_X = mybir.AxisListType.X

P = 128
T = 4
CH = T * P
U = 4
RING = U
RRING = U
FIN = 4
V_LD = 2
V_R = 1
AHEAD = 2
EPS = 1e-5


def runs(first, end):
    trips = max(end - first, 0) // U
    looped = trips if trips > 1 else 0
    return ([(first, looped)] if looped else []) + [(k, 0) for k in range(first + looped * U, end)]


def each(eng, spans, body):
    for base, trips in spans:
        if trips:
            with eng.Fori(0, trips) as q:
                for i in range(base, base + U):
                    body(i, q)
        else:
            body(base, 0)


def resnorm_gnn(nc, x, adj, W, b, out):
    N, F = x.shape
    G = N // CH
    assert F == P and tuple(adj.shape) == (N, N) and N % CH == 0 and G > 2 * U
    LAST = G - 1

    def unit_row(g):
        return g * g

    def unit_d(g):
        return g * g + g

    def unit_c(g):
        return g * g + g + 1

    def l_before(g):
        return g * (g - 1) // 2

    def summed_before(g):
        return g * (g + 1) // 2

    def r_count(g):
        return G - 1 - g

    def r_before(g):
        return sum(r_count(h) for h in range(g))

    def r_shared_before(g):
        return max(r_before(g) - r_count(0), 0)

    x_g = x.rearrange("(g t p) f -> g p t f", p=P, t=T)
    out_g = out.rearrange("(g t p) f -> g p t f", p=P, t=T)

    def group(ap, g):
        return ap[g] if isinstance(g, int) else ap[bass.ds(g, 1)].rearrange("a p t f -> (a p) t f")

    def chunk(g, c):
        return adj[bass.ds(g * CH, CH), bass.ds(c * CH, CH)].rearrange("(t p) c -> p t c", p=P)

    with ExitStack() as ctx:
        def sb(name, shape, dtype=F32):
            return ctx.enter_context(nc.sbuf_tensor(name, shape, dtype))

        def sem(name):
            return ctx.enter_context(nc.semaphore(name))

        def bank(name, n):
            return ctx.enter_context(nc.psum_tensor(name, [P, n, CH], F32))

        ring = sb("ring", [P, RING, T, CH])
        r_ring = sb("r_ring", [P, RRING, T, CH])
        support = sb("support", [P, G, T, F])
        y_acc = sb("y_acc", [P, G, CH])
        a_hi = sb("a_hi", [P, T, CH], F32R)
        a_lo = sb("a_lo", [P, T, CH], F32R)
        l_hi = sb("l_hi", [P, 2, T, F], F32R)
        l_lo = sb("l_lo", [P, 2, T, F], F32R)
        d_hi = sb("d_hi", [P, 2, T, F], F32R)
        d_lo = sb("d_lo", [P, 2, T, F], F32R)
        unused = sb("unused", [P, T, CH], BF16)
        part = sb("part", [P, 2, T, G])
        row_sum = sb("row_sum", [P, 2, T])
        deg = sb("deg", [P, G, T])
        dinv = sb("dinv", [P, G, T])
        neg_half = sb("neg_half", [P, T])
        ident = sb("ident", [P, P])
        w_rows = sb("w_rows", [P, F])
        w_t = sb("w_t", [P, F])
        ones = sb("ones", [1, P])
        bias = sb("bias", [1, F])
        x_rows = sb("x_rows", [P, FIN, T, F])
        x_t = sb("x_t", [P, 2, CH])
        y_last = sb("y_last", [P, 2, CH])
        z = sb("z", [P, FIN, T, F])
        stats = sb("stats", [P, 2, T, 6])
        halves = sb("halves", [P, FIN, 3, T])
        diff_sq = sb("diff_sq", [P, T])
        diff_var = sb("diff_var", [P, T])
        half_var = sb("half_var", [P, T])
        var_eps = sb("var_eps", [P, T])
        neg_mean = sb("neg_mean", [P, T])
        rstd = sb("rstd", [P, FIN, T])
        shift = sb("shift", [P, FIN, T])
        y_out = sb("y_out", [P, 2, T, F])

        ps_t = bank("ps_t", T)
        ps_row = bank("ps_row", 1)
        ps_col = bank("ps_col", 2)
        ps_fin = bank("ps_fin", 1)

        const_in = sem("const_in")
        x_in = [sem(f"x_in{k}") for k in range(FIN)]
        ring_in = [sem(f"ring_in{k}") for k in range(RING)]
        r_in = [sem(f"r_in{k}") for k in range(RRING)]
        stored = [sem(f"stored{k}") for k in range(2)]
        zeroed = sem("zeroed")
        const_set = sem("const_set")
        wt_done = sem("wt_done")
        wt_copied = sem("wt_copied")
        xt_done = sem("xt_done")
        xt_copied = sem("xt_copied")
        sup_done = sem("sup_done")
        sup_copied = sem("sup_copied")
        trans_done = sem("trans_done")
        hi_done = sem("hi_done")
        lo_done = sem("lo_done")
        mm_done = sem("mm_done")
        ld_sum_v = sem("ld_sum_v")
        ld_sum_a = sem("ld_sum_a")
        r0_sum = sem("r0_sum")
        r_sum_v = sem("r_sum_v")
        r_sum_a = sem("r_sum_a")
        row_summed = sem("row_summed")
        deg_ready = sem("deg_ready")
        dinv_ready = sem("dinv_ready")
        ds_ready = sem("ds_ready")
        d_hi_ready = sem("d_hi_ready")
        d_lo_ready = sem("d_lo_ready")
        l_hi_ready = sem("l_hi_ready")
        l_lo_ready = sem("l_lo_ready")
        row_saved = sem("row_saved")
        col_added = sem("col_added")
        y_turned = sem("y_turned")
        y_read = sem("y_read")
        pool_step = sem("pool_step")
        z_scaled = sem("z_scaled")
        z_ready = sem("z_ready")
        stats_step = sem("stats_step")
        stats_ready = sem("stats_ready")
        scale_ready = sem("scale_ready")
        normed = sem("normed")

        block = ctx.enter_context(nc.Block())

        def ring_at(s0, i):
            return (s0 + i) % RING

        def ring_landed(eng, s0, i, q):
            eng.wait_ge(ring_in[ring_at(s0, i)], (q + ((s0 + i) // RING + 1)) * 16)

        def r_landed(eng, n0, i, q):
            eng.wait_ge(r_in[(n0 + i) % RRING], (q + ((n0 + i) // RRING + 1)) * 16)

        @block.sync
        def _(sp):
            def load_ring(g, c, s0, i, q, summed):
                if not isinstance(summed, int) or summed > 0:
                    sp.wait_ge(ld_sum_v, summed)
                    sp.wait_ge(ld_sum_a, summed)
                if s0 + i >= RING:
                    sp.wait_ge(trans_done, (q * U + (s0 + i - RING + 1)) * T)
                slot = ring_at(s0, i)
                sp.dma_start(ring[:, slot], chunk(g, c)).then_inc(ring_in[slot], 16)

            def load_ld(g):
                def body(i, q):
                    n = summed_before(g) + (i - RING + 1 if i >= RING else 0)
                    need = q * U + n if i >= RING else n
                    load_ring(g, q * U + i, unit_row(g), i, q, need)
                return body

            def load_c(g):
                def body(i, q):
                    load_ring(q * U + i, g, unit_c(g), i, q, summed_before(g) + min(max(g + 2 + i - RING, 0), g + 1))
                return body

            def load_r(g):
                def body(i, q):
                    n0 = r_before(g)
                    if n0 + i >= RRING:
                        shared = r_shared_before(g) + i - RRING + 1
                        if g == 0 or shared <= 0:
                            sp.wait_ge(r0_sum, q * U + (n0 + i - RRING + 1))
                        else:
                            sp.wait_ge(r_sum_v, q * U + shared)
                            sp.wait_ge(r_sum_a, q * U + shared)
                    slot = (n0 + i) % RRING
                    sp.dma_start(r_ring[:, slot], chunk(g, q * U + (i + g + 1))).then_inc(r_in[slot], 16)
                return body

            sp.dma_start(w_rows[:], W).then_inc(const_in, 16)
            sp.dma_start(bias[:], b.rearrange("(a f) -> a f", a=1)).then_inc(const_in, 16)
            load_ld(0)(0, 0)
            each(sp, [(k, 0) for k in range(RRING)] + runs(RRING, r_count(0)), load_r(0))
            for g in range(G):
                if g > 0:
                    each(sp, [(k, 0) for k in range(1, min(g, RING))] + runs(RING, g), load_ld(g))
                    load_ld(g)(g, 0)
                both = min(g, r_count(g + 1)) if g < LAST else 0
                peeled = min(g, RING)
                each(sp, [(k, 0) for k in range(min(both, RING))] + runs(RING, both),
                     lambda i, q: (load_c(g)(i, q), load_r(g + 1)(i, q)))
                each(sp, [(k, 0) for k in range(both, peeled)] + runs(max(both, peeled), g), load_c(g))
                if g < LAST:
                    load_ld(g + 1)(0, 0)
                    first = RRING if g == 0 else 0
                    each(sp, [(k, 0) for k in range(first)] + runs(max(both, first), r_count(g + 1)), load_r(g + 1))

        @block.gpsimd
        def _(pool):
            nc.gpsimd.memset(ident[:], 0.0).then_inc(zeroed, 1)
            nc.gpsimd.memset(ones[:], 1.0).then_inc(const_set, 1)
            nc.gpsimd.memset(neg_half[:], -0.5).then_inc(const_set, 1)
            pool.wait_ge(zeroed, 1)
            nc.gpsimd.affine_select(out=ident[:], in_=ident[:], compare_op=ALU.not_equal, fill=1.0, base=0,
                                    pattern=[[-1, P]], channel_multiplier=1).then_inc(const_set, 1)
            pool.wait_ge(const_set, 3)

            for g in range(G):
                def stage_lo(i, q):
                    slot = (l_before(g) + i) % 2
                    pool.wait_ge(l_hi_ready, q * U + (l_before(g) + i + 1))
                    nc.gpsimd.tensor_tensor(l_lo[:, slot],
                                            support[:, bass.ds(q * U + i, 1)].rearrange("p a t f -> p (a t) f"),
                                            l_hi[:, slot].bitcast(F32), ALU.subtract).then_inc(l_lo_ready, 1)

                each(pool, runs(0, g), stage_lo)
                pool.wait_ge(deg_ready, g + 1)
                nc.gpsimd.tensor_tensor(dinv[:, g], deg[:, g], neg_half[:], ALU.pow).then_inc(dinv_ready, 1)
                pool.wait_ge(dinv_ready, g + 1)
                if g == 0:
                    pool.wait_ge(sup_copied, G)
                nc.gpsimd.tensor_tensor(support[:, g], support[:, g],
                                        dinv[:, g].unsqueeze(2).to_broadcast([P, T, F]), ALU.mult)\
                  .then_inc(ds_ready, 1)

            def add_x(e):
                row, slot = (e - 1) % G, e % FIN
                pool.wait_ge(y_read, e + 1)
                nc.gpsimd.tensor_tensor(z[:, slot], z[:, slot], dinv[:, row].unsqueeze(2).to_broadcast([P, T, F]),
                                        ALU.mult).then_inc(z_scaled, 1)
                pool.wait_ge(z_scaled, e + 1)
                pool.wait_ge(x_in[slot], ((G + e) // FIN + 1) * 16)
                nc.gpsimd.tensor_tensor(z[:, slot], z[:, slot], x_rows[:, slot], ALU.add).then_inc(z_ready, 1)

            def scale(e):
                slot = e % FIN
                pool.wait_ge(stats_ready, e + 1)
                if e >= FIN:
                    pool.wait_ge(normed, e - FIN + 1)
                if e >= 1:
                    pool.wait_ge(scale_ready, e)
                nc.gpsimd.tensor_scalar(neg_mean[:], halves[:, slot, 0], -0.5, None, ALU.mult).then_inc(pool_step, 1)
                nc.gpsimd.tensor_scalar(half_var[:], halves[:, slot, 2], 1.0 / F, EPS, ALU.mult, ALU.add)\
                  .then_inc(pool_step, 1)
                nc.gpsimd.tensor_tensor(diff_sq[:], halves[:, slot, 1], halves[:, slot, 1], ALU.mult)\
                  .then_inc(pool_step, 1)
                pool.wait_ge(pool_step, 6 * e + 3)
                nc.gpsimd.tensor_scalar(diff_var[:], diff_sq[:], 0.25, None, ALU.mult).then_inc(pool_step, 1)
                pool.wait_ge(pool_step, 6 * e + 4)
                nc.gpsimd.tensor_tensor(var_eps[:], diff_var[:], half_var[:], ALU.add).then_inc(pool_step, 1)
                pool.wait_ge(pool_step, 6 * e + 5)
                nc.gpsimd.tensor_tensor(rstd[:, slot], var_eps[:], neg_half[:], ALU.pow).then_inc(pool_step, 1)
                pool.wait_ge(pool_step, 6 * e + 6)
                nc.gpsimd.tensor_tensor(shift[:, slot], neg_mean[:], rstd[:, slot], ALU.mult).then_inc(scale_ready, 1)

            for e in range(G):
                add_x(e)
                if e >= 1:
                    scale(e - 1)
            scale(G - 1)

        @block.scalar
        def _(act):
            def load_x(k, slot):
                act.dma_start(x_rows[:, slot], group(x_g, k)).then_inc(x_in[slot], 16)

            for k in range(FIN):
                load_x(k, k)
            act.wait_ge(wt_done, 1)
            nc.scalar.copy(w_t[:], ps_fin[:, 0, 0:F]).then_inc(wt_copied, 1)

            def copy_x(i, q, more):
                act.wait_ge(xt_done, q * U + i + 1)
                if i >= 2:
                    act.wait_ge(sup_done, q * U + (i - 1))
                nc.scalar.copy(x_t[:, i % 2], ps_t[:, i % 2]).then_inc(xt_copied, 1)
                if more:
                    load_x(q * U + (i + FIN), i % FIN)

            def copy_support(i, q):
                act.wait_ge(sup_done, q * U + i + 1)
                nc.scalar.copy(support[:, bass.ds(q * U + i, 1)].rearrange("p a t f -> p (a t f)"),
                               ps_t[:, 2 + i % 2]).then_inc(sup_copied, 1)

            copy_x(0, 0, True)
            each(act, [(0, 0)] + runs(1, G - FIN - 1), lambda i, q: (copy_x(i + 1, q, True), copy_support(i, q)))
            for k in range(G - FIN - 1, G - 1):
                copy_x(k + 1, 0, False)
                copy_support(k, 0)
            copy_support(G - 1, 0)

            def part_at(g, c, t):
                return part[:, g % 2, t, bass.ds(c, 1)]

            def sum_share(chunk_in, g, c, first, summed, before, landed):
                def step(t):
                    if t == first:
                        if not isinstance(before, int) or before > 0:
                            act.wait_ge(summed, before)
                        landed()
                    done = nc.scalar.activation(unused[:, t], chunk_in[:, t], ACT.Copy,
                                                accum_out=part_at(g, c, t))
                    if t == T - 1:
                        done.then_inc(summed, 1)
                return [lambda t=t: step(t) for t in range(first, T)]

            def sum_ld(g, i, q):
                if r_shared_before(g + 1):
                    act.wait_ge(r_sum_a, r_shared_before(g + 1))
                return sum_share(ring[:, ring_at(unit_row(g), i)], g, q * U + i, V_LD, ld_sum_a,
                                 q * U + (summed_before(g) + i), lambda: ring_landed(act, unit_row(g), i, q))

            def sum_r(g, i, q):
                n0 = r_before(g)
                act.wait_ge(ld_sum_a, summed_before(g))
                return sum_share(r_ring[:, (n0 + i) % RRING], g, q * U + (i + g + 1), V_R, r_sum_a,
                                 q * U + (r_shared_before(g) + i), lambda: r_landed(act, n0, i, q))

            def stage_hi(g, i, q):
                if i + l_before(g) >= 2:
                    last = (unit_row(g) + i - 1) if i >= 2 else unit_d(g - 1)
                    act.wait_ge(mm_done, (q * U + last) * T)
                if i == 0:
                    act.wait_ge(ds_ready, g)
                nc.scalar.copy(l_hi[:, (l_before(g) + i) % 2],
                               support[:, bass.ds(q * U + i, 1)].rearrange("p a t f -> p (a t) f"))\
                  .then_inc(l_hi_ready, 1)

            def evac(s0, i, q, j):
                act.wait_ge(trans_done, (q * U + (s0 + i)) * T + (j + 1))
                if s0 + i >= 1:
                    act.wait_ge(mm_done, (q * U + (s0 + i - 1)) * T + (j + 1))
                nc.scalar.copy(a_hi[:, j], ps_t[:, j]).then_inc(hi_done, 1)

            def unit(s0, i, q, more=True, steps=()):
                steps = list(steps)
                for n, j in enumerate((2, 3, 0, 1)):
                    if n < 2 or more:
                        evac(s0, i + n // 2, q, j)
                    if n < len(steps) and steps[n]:
                        steps[n]()
                for step in steps[T:]:
                    step()

            def unit_l(g):
                def body(i, q):
                    unit(unit_row(g), i, q, True, [lambda: stage_hi(g, i + 1, q), *sum_ld(g, i + AHEAD, q)])
                return body

            def split_ds(g):
                act.wait_ge(ds_ready, g + 1)
                if g >= 2:
                    act.wait_ge(mm_done, unit_row(g - 1) * T)
                nc.scalar.copy(d_hi[:, g % 2], support[:, g]).then_inc(d_hi_ready, 1)

            evac(0, 0, 0, 0)
            evac(0, 0, 0, 1)
            for step in sum_ld(0, 0, 0):
                step()
            for g in range(G):
                if g > 0:
                    each(act, runs(0, g - 1), unit_l(g))
                    unit(unit_row(g), g - 1, 0, True, [None, None, lambda: split_ds(g)])
                else:
                    split_ds(g)
                unit(unit_d(g), 0, 0)
                act.wait_ge(mm_done, (unit_d(g) + 1) * T)
                nc.scalar.copy(y_acc[:, g] if g < LAST else y_last[:, 0], ps_row[:, 0]).then_inc(row_saved, 1)
                if g < LAST:
                    stage_hi(g + 1, 0, 0)
                    both = min(g, r_count(g + 1))
                    early = both <= g - AHEAD
                    each(act, runs(0, both), lambda i, q: unit(unit_c(g), i, q, True, sum_r(g + 1, i, q)))
                    each(act, runs(both, g - AHEAD if early else g), lambda i, q: unit(unit_c(g), i, q))
                    each(act, runs(both, r_count(g + 1)), lambda i, q: [step() for step in sum_r(g + 1, i, q)])
                    for c in range(AHEAD):
                        if early:
                            unit(unit_c(g), g - AHEAD + c, 0, True, sum_ld(g + 1, c, 0))
                        else:
                            for step in sum_ld(g + 1, c, 0):
                                step()

            def fin_row(i, q):
                return LAST if (isinstance(q, int) and i == 0) else q * U + (i - 1)

            def load_res(i, q):
                slot = i % FIN
                act.dma_start(x_rows[:, slot], group(x_g, fin_row(i, q))).then_inc(x_in[slot], 16)

            def norm(i, q, more):
                slot = i % FIN
                act.wait_ge(scale_ready, q * U + i + 1)
                if i >= 2:
                    act.wait_ge(stored[i % 2], (q * (U // 2) + (i - 2) // 2 + 1) * 16)
                for t in range(T):
                    done = nc.scalar.activation(y_out[:, i % 2, t], z[:, slot, t], ACT.Identity,
                                                bias=shift[:, slot, t:t + 1], scale=rstd[:, slot, t:t + 1])
                done.then_inc(normed, 1)
                if more:
                    load_res(i + FIN, q)
                act.wait_ge(normed, q * U + i + 1)
                act.dma_start(group(out_g, fin_row(i, q)), y_out[:, i % 2]).then_inc(stored[i % 2], 16)

            for e in range(FIN):
                load_res(e, 0)
            s0 = unit_c(LAST)
            LAG = 3
            for k in range(LAG + 2):
                unit(s0, k, 0)
                if k >= LAG:
                    norm(k - LAG, 0, True)
            each(act, runs(LAG + 2, LAST - 1),
                 lambda i, q: (unit(s0, i, q), norm(i - LAG, q, True)))
            unit(s0, LAST - 1, 0, False)
            for e in range(LAST - 1 - LAG, G):
                norm(e, 0, e + FIN < G)
            act.wait_ge(stored[0], G // 2 * 16)
            act.wait_ge(stored[1], G // 2 * 16)

        @block.vector
        def _(dve):
            def sum_ld(g, i, q):
                ring_landed(dve, unit_row(g), i, q)
                nc.vector.tensor_reduce(part[:, g % 2, 0:V_LD, bass.ds(q * U + i, 1)].rearrange("p t a -> p (t a)"),
                                        ring[:, ring_at(unit_row(g), i), 0:V_LD], AX_X, ALU.add).then_inc(ld_sum_v, 1)

            def sum_r(g):
                def body(i, q):
                    n0 = r_before(g)
                    r_landed(dve, n0, i, q)
                    share = V_R if g else T
                    nc.vector.tensor_reduce(
                        part[:, g % 2, 0:share, bass.ds(q * U + (i + g + 1), 1)].rearrange("p t a -> p (t a)"),
                        r_ring[:, (n0 + i) % RRING, 0:share], AX_X, ALU.add).then_inc(r_sum_v if g else r0_sum, 1)
                return body

            def lo(s0, i, q, j):
                dve.wait_ge(hi_done, (q * U + (s0 + i)) * T + (j + 1))
                nc.vector.tensor_tensor(a_lo[:, j], ps_t[:, j], a_hi[:, j].bitcast(F32), ALU.subtract)\
                  .then_inc(lo_done, 1)

            def unit(s0, i, q, more=True, after_2=None, after_3=None):
                lo(s0, i, q, 2)
                if after_2:
                    after_2()
                lo(s0, i, q, 3)
                if after_3:
                    after_3()
                if more:
                    lo(s0, i + 1, q, 0)
                    lo(s0, i + 1, q, 1)

            def unit_l(g):
                def body(i, q):
                    unit(unit_row(g), i, q, True, lambda: sum_ld(g, i + AHEAD, q))
                return body

            def total(g):
                dve.wait_ge(ld_sum_v, summed_before(g + 1))
                dve.wait_ge(ld_sum_a, summed_before(g + 1))
                if g == 0:
                    dve.wait_ge(r0_sum, r_count(0))
                else:
                    dve.wait_ge(r_sum_v, r_shared_before(g + 1))
                    dve.wait_ge(r_sum_a, r_shared_before(g + 1))
                nc.vector.tensor_reduce(row_sum[:, g % 2], part[:, g % 2], AX_X, ALU.add).then_inc(row_summed, 1)
                dve.wait_ge(row_summed, g + 1)
                nc.vector.tensor_scalar(deg[:, g], row_sum[:, g % 2], 1.0, None, ALU.add).then_inc(deg_ready, 1)

            def split_ds(g):
                dve.wait_ge(d_hi_ready, g + 1)
                nc.vector.tensor_tensor(d_lo[:, g % 2], support[:, g], d_hi[:, g % 2].bitcast(F32), ALU.subtract)\
                  .then_inc(d_lo_ready, 1)

            def add_c(g):
                def body(i, q):
                    n = l_before(g) + i
                    dve.wait_ge(mm_done, (q * U + (unit_c(g) + i + 1)) * T)
                    rows = y_acc[:, bass.ds(q * U + i, 1)].rearrange("p a c -> p (a c)")
                    to = rows if g < LAST else y_last[:, (i + 1) % 2]
                    nc.vector.tensor_tensor(to, rows, ps_col[:, n % 2], ALU.add).then_inc(col_added, 1)
                return body

            each(dve, runs(0, r_count(0)), sum_r(0))
            lo(0, 0, 0, 0)
            lo(0, 0, 0, 1)
            sum_ld(0, 0, 0)
            for g in range(G):
                if g > 0:
                    each(dve, runs(0, g - 1), unit_l(g))
                    total(g)
                    unit(unit_row(g), g - 1, 0)
                else:
                    total(g)
                split_ds(g)
                unit(unit_d(g), 0, 0)
                if g > 0:
                    dve.wait_ge(row_saved, g)
                    dve.wait_ge(col_added, l_before(g))
                if g < LAST:
                    both = min(g, r_count(g + 1))
                    early = both <= g - AHEAD
                    each(dve, runs(0, both),
                         lambda i, q: (unit(unit_c(g), i, q, True, lambda: sum_r(g + 1)(i, q)), add_c(g)(i, q)))
                    each(dve, runs(both, g - AHEAD if early else g),
                         lambda i, q: (unit(unit_c(g), i, q), add_c(g)(i, q)))
                    each(dve, runs(both, r_count(g + 1)), sum_r(g + 1))
                    for c in range(AHEAD):
                        if early:
                            unit(unit_c(g), g - AHEAD + c, 0, True, lambda: sum_ld(g + 1, c, 0))
                            add_c(g)(g - AHEAD + c, 0)
                        else:
                            sum_ld(g + 1, c, 0)

            def read_y(i, q):
                slot = i % FIN
                row = LAST if (isinstance(q, int) and i == 0) else q * U + (i - 1)
                e = q * U + i
                if i >= FIN:
                    dve.wait_ge(normed, e - (FIN - 1))
                dve.wait_ge(y_turned, e + 1)
                ds = support[:, bass.ds(row, 1)].rearrange("p a t f -> p (a t) f")
                turned = ps_fin[:, 0].rearrange("p (t f) -> p t f", f=F)
                nc.vector.tensor_tensor(z[:, slot], turned, ds, ALU.add).then_inc(y_read, 1)

            def halve(i, q):
                slot = i % FIN
                e = q * U + i
                dve.wait_ge(z_ready, e + 1)
                for t in range(T):
                    done = nc.vector.bn_stats(stats[:, i % 2, t], z[:, slot, t])
                done.then_inc(stats_step, 1)
                dve.wait_ge(stats_step, e + 1)
                mean_e, mean_o = stats[:, i % 2, :, 1], stats[:, i % 2, :, 4]
                nc.vector.tensor_tensor(halves[:, slot, 0], mean_e, mean_o, ALU.add)
                nc.vector.tensor_tensor(halves[:, slot, 1], mean_e, mean_o, ALU.subtract)
                nc.vector.tensor_tensor(halves[:, slot, 2], stats[:, i % 2, :, 2], stats[:, i % 2, :, 5], ALU.add)\
                  .then_inc(stats_ready, 1)

            def last(i, q, more=True):
                if i >= 2:
                    dve.wait_ge(y_turned, q * U + i)
                unit(unit_c(LAST), i, q, more)
                add_c(LAST)(i, q)
                if i >= 1:
                    halve(i - 1, q)
                read_y(i, q)

            each(dve, [(k, 0) for k in range(5)] + runs(5, LAST - 1), last)
            last(LAST - 1, 0, False)
            halve(LAST - 1, 0)
            read_y(LAST, 0)
            halve(LAST, 0)

        @block.tensor
        def _(pe):
            pe.wait_ge(const_in, 32)
            pe.wait_ge(const_set, 3)
            nc.tensor.transpose(ps_fin[:, 0, 0:F], w_rows[:], ident[:]).then_inc(wt_done, 1)

            def turn_x(i, q):
                slot = i % 2
                pe.wait_ge(x_in[i % FIN], (q + (i // FIN + 1)) * 16)
                if i >= 2:
                    pe.wait_ge(xt_copied, q * U + (i - 1))
                for t in range(T):
                    done = nc.tensor.transpose(ps_t[:, slot, t * P:(t + 1) * P], x_rows[:, i % FIN, t], ident[:])
                done.then_inc(xt_done, 1)

            def mul_x(i, q):
                slot = i % 2
                pe.wait_ge(xt_copied, q * U + i + 1)
                if i >= 2:
                    pe.wait_ge(sup_copied, q * U + (i - 1))
                for t in range(T):
                    to = ps_t[:, 2 + slot, t * F:(t + 1) * F]
                    nc.tensor.matmul(to, x_t[:, slot, t * P:(t + 1) * P], w_t[:], start=True, stop=False)
                    done = nc.tensor.matmul(to, ones[:], bias[:], start=False, stop=True)
                done.then_inc(sup_done, 1)

            turn_x(0, 0)
            pe.wait_ge(wt_copied, 1)
            each(pe, [(0, 0)] + [(k, 0) for k in range(1, 3)] + runs(3, G - 1),
                 lambda i, q: (turn_x(i + 1, q), mul_x(i, q)))
            mul_x(G - 1, 0)
            pe.wait_ge(sup_copied, G)

            def turn(s0, i, q, j):
                if j == 0:
                    ring_landed(pe, s0, i, q)
                slot = ring_at(s0, i)
                for t in range(T):
                    done = nc.tensor.transpose(ps_t[:, j, t * P:(t + 1) * P],
                                               ring[:, slot, t, j * P:(j + 1) * P], ident[:])
                done.then_inc(trans_done, 1)

            def mul(s0, i, q, j, w_hi, w_lo, to, start, stop):
                pe.wait_ge(lo_done, (q * U + (s0 + i)) * T + (j + 1))
                nc.tensor.matmul(to, w_hi[:, j], a_hi[:, j], start=start, stop=False)
                nc.tensor.matmul(to, w_hi[:, j], a_lo[:, j], start=False, stop=False)
                nc.tensor.matmul(to, w_lo[:, j], a_hi[:, j], start=False, stop=stop).then_inc(mm_done, 1)

            def unit(s0, i, q, ready, w_hi, w_lo, to, opens, closes, more=True):
                turn(s0, i, q, 2)
                ready()
                mul(s0, i, q, 0, w_hi, w_lo, to, opens, False)
                turn(s0, i, q, 3)
                mul(s0, i, q, 1, w_hi, w_lo, to, False, False)
                if more:
                    turn(s0, i + 1, q, 0)
                mul(s0, i, q, 2, w_hi, w_lo, to, False, False)
                if more:
                    turn(s0, i + 1, q, 1)
                mul(s0, i, q, 3, w_hi, w_lo, to, False, closes)

            def unit_of_l(g):
                def body(i, q):
                    n = l_before(g) + i

                    def ready():
                        pe.wait_ge(l_lo_ready, q * U + (n + 1))
                        if i == 0:
                            pe.wait_ge(row_saved, g)
                    unit(unit_row(g), i, q, ready, l_hi[:, n % 2], l_lo[:, n % 2], ps_row[:, 0], i == 0, False)
                return body

            def unit_of_c(g, more=True):
                def body(i, q):
                    n = l_before(g) + i

                    def ready():
                        if n >= 2:
                            pe.wait_ge(col_added, q * U + (n - 1))
                    unit(unit_c(g), i, q, ready, d_hi[:, g % 2], d_lo[:, g % 2], ps_col[:, n % 2], True, True, more)
                return body

            turn(0, 0, 0, 0)
            turn(0, 0, 0, 1)
            for g in range(G):
                if g > 0:
                    each(pe, [(0, 0)] + runs(1, g), unit_of_l(g))
                unit(unit_d(g), 0, 0, lambda: pe.wait_ge(d_lo_ready, g + 1), d_hi[:, g % 2], d_lo[:, g % 2], ps_row[:, 0], g == 0, True)
                if g < LAST:
                    each(pe, runs(0, g), unit_of_c(g))

            def turn_back(i, q):
                e = q * U + i
                if i == 0:
                    pe.wait_ge(row_saved, G)
                else:
                    pe.wait_ge(col_added, e + l_before(LAST))
                    pe.wait_ge(y_read, e)
                for t in range(T):
                    done = nc.tensor.transpose(ps_fin[:, 0, t * P:(t + 1) * P],
                                               y_last[:, i % 2, t * P:(t + 1) * P], ident[:])
                done.then_inc(y_turned, 1)

            each(pe, [(0, 0)] + runs(1, LAST - 1), lambda i, q: (unit_of_c(LAST)(i, q), turn_back(i, q)))
            unit_of_c(LAST, False)(LAST - 1, 0)
            turn_back(LAST - 1, 0)
            turn_back(LAST, 0)


_INS = ['x', 'adj', 'L0_gnn_W', 'L0_gnn_b']


def kernel(**inputs):
    import numpy as _np
    import concourse.bacc as _bacc
    from concourse import mybir as _mybir
    from concourse.bass_utils import run_bass_kernel_spmd as _run

    nc = _bacc.Bacc("TRN2", target_bir_lowering=False, num_devices=1)
    arrays, args = {}, []
    for name in _INS:
        a = _np.ascontiguousarray(inputs[name])
        arrays[f"in_{name}_dram"] = a
        args.append(nc.dram_tensor(f"in_{name}_dram", a.shape, _mybir.dt.from_np(a.dtype), kind="ExternalInput").ap())
    x = arrays["in_x_dram"]
    args.append(nc.dram_tensor("out_0_dram", x.shape, _mybir.dt.from_np(x.dtype), kind="ExternalOutput").ap())
    resnorm_gnn(nc, *args)
    r = _run(nc, [arrays], core_ids=[0])
    return r.results[0]["out_0_dram"]
```

```python
from contextlib import ExitStack

import concourse.bass as bass
from concourse import mybir

F32 = mybir.dt.float32
F32R = mybir.dt.float32r
BF16 = mybir.dt.bfloat16
ALU = mybir.AluOpType
ACT = mybir.ActivationFunctionType
AX_X = mybir.AxisListType.X

P = 128
T = 4
CH = T * P
U = 4
RING = U
RRING = 4
KEEP = 1
FAR_ROWS = 6
FIN = 4
V_LD = 2
V_R = 1
AHEAD = 2
DENSE_ROWS = 5
LAG = 2
R_FIRST = 1
EPS = 1e-5


def runs(first, end):
    trips = max(end - first, 0) // U
    looped = trips if trips > 1 else 0
    return ([(first, looped)] if looped else []) + [(k, 0) for k in range(first + looped * U, end)]


def each(eng, spans, body):
    for base, trips in spans:
        if trips:
            with eng.Fori(0, trips) as q:
                for i in range(base, base + U):
                    body(i, q)
        else:
            body(base, 0)


def resnorm_gnn(nc, x, adj, W, b, out):
    N, F = x.shape
    G = N // CH
    assert F == P and tuple(adj.shape) == (N, N) and N % CH == 0 and G > 2 * U
    LAST = G - 1

    def unit_row(g):
        return g * g

    def unit_d(g):
        return g * g + g

    def unit_c(g):
        return g * g + g + 1

    def l_before(g):
        return g * (g - 1) // 2

    def summed_before(g):
        return g * (g + 1) // 2

    def r_ringed(g):
        return G - 1 - g - r_kept(g)

    def r_kept(g):
        return min(G - 1 - g, KEEP + (1 if g < FAR_ROWS else 0))

    def r_ringed_before(g):
        return sum(r_ringed(h) for h in range(g))

    def r_shared_before(g):
        return sum(r_ringed(h) + r_kept(h) for h in range(1, g))

    def c_kept(g):
        return sum(1 for h in range(g) if g - h <= r_kept(h))

    def ring_row(g):
        return g * g - sum(c_kept(h) for h in range(g))

    def ring_c(g):
        return ring_row(g) + g + 1

    def ring_unit(r):
        g = max(h for h in range(G) if ring_row(h) <= r)
        k = r - ring_row(g)
        return g, k, unit_row(g) + k + (c_kept(g) if k > g else 0)

    def c_row(g, i, q):
        return g - 1 - i if i < c_kept(g) and isinstance(q, int) else q * U + (i - c_kept(g))

    x_g = x.rearrange("(g t p) f -> g p t f", p=P, t=T)
    out_g = out.rearrange("(g t p) f -> g p t f", p=P, t=T)

    def group(ap, g):
        return ap[g] if isinstance(g, int) else ap[bass.ds(g, 1)].rearrange("a p t f -> (a p) t f")

    def chunk(g, c):
        return adj[bass.ds(g * CH, CH), bass.ds(c * CH, CH)].rearrange("(t p) c -> p t c", p=P)

    with ExitStack() as ctx:
        def sb(name, shape, dtype=F32):
            return ctx.enter_context(nc.sbuf_tensor(name, shape, dtype))

        def sem(name):
            return ctx.enter_context(nc.semaphore(name))

        def bank(name, n):
            return ctx.enter_context(nc.psum_tensor(name, [P, n, CH], F32))

        ring = sb("ring", [P, RING, T, CH])
        r_ring = sb("r_ring", [P, RRING, T, CH])
        support = sb("support", [P, G, T, F])
        y_acc = sb("y_acc", [P, LAST, CH])
        a_hi = sb("a_hi", [P, T, CH], F32R)
        a_lo = sb("a_lo", [P, T, CH], F32R)
        l_hi = sb("l_hi", [P, 2, T, F], F32R)
        l_lo = sb("l_lo", [P, 2, T, F], F32R)
        d_hi = sb("d_hi", [P, T, F], F32R)
        d_lo = sb("d_lo", [P, T, F], F32R)
        unused_r = sb("unused_r", [P, T - V_R, CH], BF16)
        unused_ld = sb("unused_ld", [P, T - V_LD, CH], BF16)
        part = sb("part", [P, 2, T, G])
        row_sum = sb("row_sum", [P, 2, T])
        deg = sb("deg", [P, G, T])
        dinv = sb("dinv", [P, G, T])
        neg_half = sb("neg_half", [P, T])
        ident = sb("ident", [P, P])
        w_rows = sb("w_rows", [P, F])
        w_t = sb("w_t", [P, F])
        bias = sb("bias", [P, F])
        x_rows = sb("x_rows", [P, FIN, T, F])
        result = sb("result", [P, 2, T, F])
        flip = sb("flip", [P, 2, CH])
        kept = sb("kept", [P, 2, T, CH])
        own_share = sb("own_share", [P, T, F])
        stats = sb("stats", [P, 2, T, 6])
        halves = sb("halves", [P, FIN, 3, T])
        diff_sq = sb("diff_sq", [P, T])
        m2_part = sb("m2_part", [P, T])
        var4 = sb("var4", [P, T])
        half_rstd = sb("half_rstd", [P, T])
        rstd = sb("rstd", [P, FIN, T])
        shift = sb("shift", [P, FIN, T])

        ps_t = bank("ps_t", T)
        ps_row = bank("ps_row", 1)
        ps_col = bank("ps_col", 2)
        ps_fin = bank("ps_fin", 1)

        const_in = sem("const_in")
        x_in = [sem(f"x_in{k}") for k in range(FIN)]
        ring_in = [sem(f"ring_in{k}") for k in range(RING)]
        r_in = [sem(f"r_in{k}") for k in range(RRING)]
        kept_in = [sem(f"kept_in{k}") for k in range(2)]
        far_in = [sem(f"far_in{k}") for k in range(3)]
        stored = [sem(f"stored{k}") for k in range(2)]
        zeroed = sem("zeroed")
        const_set = sem("const_set")
        wt_done = sem("wt_done")
        wt_copied = sem("wt_copied")
        xt_done = sem("xt_done")
        xt_copied = sem("xt_copied")
        sup_done = sem("sup_done")
        sup_copied = sem("sup_copied")
        trans_done = sem("trans_done")
        hi_done = sem("hi_done")
        lo_done = sem("lo_done")
        mm_done = sem("mm_done")
        ld_sum_v = sem("ld_sum_v")
        ld_sum_a = sem("ld_sum_a")
        r0_sum = sem("r0_sum")
        r_sum_v = sem("r_sum_v")
        r_sum_a = sem("r_sum_a")
        row_summed = sem("row_summed")
        deg_ready = sem("deg_ready")
        dinv_ready = sem("dinv_ready")
        ds_ready = sem("ds_ready")
        d_hi_ready = sem("d_hi_ready")
        d_lo_ready = sem("d_lo_ready")
        l_hi_ready = sem("l_hi_ready")
        l_lo_ready = sem("l_lo_ready")
        row_saved = sem("row_saved")
        col_added = sem("col_added")
        y_turned = sem("y_turned")
        pool_step = sem("pool_step")
        own_scaled = sem("own_scaled")
        base_ready = sem("base_ready")
        z_ready = sem("z_ready")
        stats_step = sem("stats_step")
        stats_ready = sem("stats_ready")
        scale_ready = sem("scale_ready")
        normed = sem("normed")

        block = ctx.enter_context(nc.Block())

        def early(g):
            return g <= LAST and r_ringed(g) + r_kept(g) + AHEAD > g - 1

        def r_until(g, k):
            per_unit = [R_FIRST if g == 0 else 0, 1 if g < DENSE_ROWS else 0]
            per_unit += [2 if j < c_kept(g) and g < DENSE_ROWS else 1 for j in range(g)]
            return min(sum(per_unit[:k + 2]), r_ringed(g + 1) + r_kept(g + 1))

        def r_in_unit(g, k):
            return range(r_until(g, k), r_until(g, k + 1)) if early(g + 1) else ()

        def r_with_c(g):
            return r_until(g - 1, g - 1)

        def r_after_l(g):
            return min(r_with_c(g) + g, r_ringed(g) + r_kept(g))

        def total_first(g):
            return not early(g) or r_with_c(g) + g - 1 >= r_ringed(g) + r_kept(g)

        def rest_of_r(eng, g, ringed, with_kept):
            first = r_after_l(g)
            peeled = min(max(first, RRING), max(r_ringed(g), first))
            each(eng, [(k, 0) for k in range(first, min(peeled, r_ringed(g)))] + runs(peeled, r_ringed(g)), ringed)
            for m in range(max(first, r_ringed(g)), r_ringed(g) + r_kept(g)):
                with_kept(m - r_ringed(g) + 1)

        def ld_with_c(g, k):
            return [n for n in range(AHEAD) if max(g - AHEAD + n, 0) == k]

        def fin_row(i, q):
            return LAST if (isinstance(q, int) and i == 0) else c_row(LAST, i - 1, q)

        def ring_at(s0, i):
            return (s0 + i) % RING

        def ring_landed(eng, s0, i, q):
            eng.wait_ge(ring_in[ring_at(s0, i)], (q + ((s0 + i) // RING + 1)) * 16)

        def r_landed(eng, n0, i, q):
            eng.wait_ge(r_in[(n0 + i) % RRING], (q * (U // RRING) + ((n0 + i) // RRING + 1)) * 16)

        idle = LAST - 2 * T
        assert KEEP == 1 and FAR_ROWS <= idle
        far = [y_acc[:, idle:idle + T], y_acc[:, idle + T:LAST], x_rows[:].rearrange("p k t f -> p k (t f)")]

        def kept_at(g, d):
            n = g % (d + 1)
            return (kept[:, n], kept_in[n], (g // 2 + 1) * 16) if d == 1 else (far[n], far_in[n], (g // 3 + 1) * 16)

        @block.sync
        def _(sp):
            def load_ring(g, c, r0, i, q):
                if r0 + i >= RING:
                    h, k, last = ring_unit(r0 + i - RING)
                    if k <= h:
                        sp.wait_ge(ld_sum_v, q * U + (summed_before(h) + k + 1))
                        sp.wait_ge(ld_sum_a, q * U + (summed_before(h) + k + 1))
                    elif not isinstance(q, int):
                        sp.wait_ge(ld_sum_v, summed_before(h + 1))
                    sp.wait_ge(trans_done, (q * U + (last + 1)) * T)
                slot = ring_at(r0, i)
                sp.dma_start(ring[:, slot], chunk(g, c)).then_inc(ring_in[slot], 16)

            def load_ld(g):
                return lambda i, q: load_ring(g, q * U + i, ring_row(g), i, q)

            def load_c(g):
                def body(i, q):
                    if i >= c_kept(g):
                        load_ring(c_row(g, i, q), g, ring_c(g) - c_kept(g), i, q)
                return body

            def load_r(g):
                def body(i, q):
                    n0 = r_ringed_before(g)
                    if n0 + i >= RRING:
                        n = n0 + i - RRING
                        h = max(h for h in range(G) if r_ringed(h) and r_ringed_before(h) <= n)
                        count = (r_shared_before(h) if h else 0) + n - r_ringed_before(h) + 1
                        if h == 0:
                            sp.wait_ge(r0_sum, q * U + count)
                        else:
                            sp.wait_ge(r_sum_v, q * U + count)
                            sp.wait_ge(r_sum_a, q * U + count)
                    slot = (n0 + i) % RRING
                    sp.dma_start(r_ring[:, slot], chunk(g, q * U + (i + g + 1 + r_kept(g)))).then_inc(r_in[slot], 16)
                return body

            def load_kept(g, d):
                to, landed, _ = kept_at(g, d)
                if g >= d + 1:
                    sp.wait_ge(trans_done, (unit_c(g - 1) + d) * T)
                if d == 2 and g == 2:
                    sp.wait_ge(xt_done, G)
                sp.dma_start(to, chunk(g, g + d)).then_inc(landed, 16)

            sp.dma_start(w_rows[:], W).then_inc(const_in, 16)
            sp.dma_start(bias[:], b.rearrange("(a f) -> a f", a=1).to_broadcast([P, F])).then_inc(const_in, 16)
            load_ld(0)(0, 0)
            each(sp, [(k, 0) for k in range(RRING)] + runs(RRING, r_ringed(0)), load_r(0))
            for d in range(1, r_kept(0) + 1):
                load_kept(0, d)

            def load_r_or_kept(g, m):
                if m < r_ringed(g):
                    load_r(g)(m, 0)
                elif m < r_ringed(g) + r_kept(g):
                    load_kept(g, m - r_ringed(g) + 1)

            for m in range(R_FIRST):
                load_r(1)(m, 0)
            for g in range(G):
                if g > 0 and early(g):
                    for k in range(g):
                        if k + AHEAD <= g:
                            load_ld(g)(k + AHEAD, 0)
                        load_r_or_kept(g, r_with_c(g) + k)
                    rest_of_r(sp, g, load_r(g), lambda d: load_kept(g, d))
                elif g > 0:
                    each(sp, [(k, 0) for k in range(1, min(g, RING))] + runs(RING, g), load_ld(g))
                    load_ld(g)(g, 0)
                if early(g + 1):
                    loads = [(load_c(g), k) for k in range(c_kept(g), g)] + [(load_ld(g + 1), k) for k in range(AHEAD)]
                    issued = 0
                    for k in range(-1, g):
                        ahead = min(max(RING - 1 if g < DENSE_ROWS else 0, k + 1 - c_kept(g)), len(loads))
                        for load, n in loads[issued:ahead]:
                            load(n, 0)
                        issued = ahead
                        for m in r_in_unit(g, k):
                            load_r_or_kept(g + 1, m)
                    for load, n in loads[issued:]:
                        load(n, 0)
                elif g < LAST:
                    both = r_ringed(g + 1)
                    peeled = min(both, KEEP + RING)
                    each(sp, [(k, 0) for k in range(peeled)] + runs(peeled, both),
                         lambda i, q: (load_c(g)(i, q), load_r(g + 1)(i, q)))
                    hidden = g - AHEAD - KEEP
                    peeled = max(both, min(hidden, KEEP + RING))
                    each(sp, [(k, 0) for k in range(both, peeled)] + runs(peeled, hidden), load_c(g))
                    for d in range(1, r_kept(g + 1) + 1):
                        load_kept(g + 1, d)
                    for k in range(hidden, g):
                        load_c(g)(k, 0)
                    load_ld(g + 1)(0, 0)
                else:
                    each(sp, [(k, 0) for k in range(KEEP + RING)] + runs(KEEP + RING, g), load_c(g))

        @block.gpsimd
        def _(pool):
            nc.gpsimd.memset(ident[:], 0.0).then_inc(zeroed, 1)
            nc.gpsimd.memset(neg_half[:], -0.5).then_inc(const_set, 1)
            pool.wait_ge(zeroed, 1)
            nc.gpsimd.affine_select(out=ident[:], in_=ident[:], compare_op=ALU.not_equal, fill=1.0, base=0,
                                    pattern=[[-1, P]], channel_multiplier=1).then_inc(const_set, 1)
            pool.wait_ge(const_set, 2)

            for g in range(G):
                def stage_lo(i, q):
                    slot = (l_before(g) + i) % 2
                    pool.wait_ge(l_hi_ready, q * U + (l_before(g) + i + 1))
                    nc.gpsimd.tensor_tensor(l_lo[:, slot],
                                            support[:, bass.ds(q * U + i, 1)].rearrange("p a t f -> p (a t) f"),
                                            l_hi[:, slot].bitcast(F32), ALU.subtract).then_inc(l_lo_ready, 1)

                each(pool, runs(0, g), stage_lo)
                pool.wait_ge(deg_ready, g + 1)
                nc.gpsimd.tensor_tensor(dinv[:, g], deg[:, g], neg_half[:], ALU.pow).then_inc(dinv_ready, 1)
                pool.wait_ge(dinv_ready, g + 1)
                if g == 0:
                    pool.wait_ge(sup_copied, G)
                nc.gpsimd.tensor_tensor(support[:, g], support[:, g],
                                        dinv[:, g].unsqueeze(2).to_broadcast([P, T, F]), ALU.mult)\
                  .then_inc(ds_ready, 1)

            def prepare(e):
                slot = e % FIN
                rows = fin_row(e, 0)
                if e >= 1:
                    pool.wait_ge(base_ready, e)
                nc.gpsimd.tensor_tensor(own_share[:], support[:, rows],
                                        dinv[:, rows].unsqueeze(2).to_broadcast([P, T, F]),
                                        ALU.mult).then_inc(own_scaled, 1)
                pool.wait_ge(own_scaled, e + 1)
                pool.wait_ge(x_in[slot], ((G + e) // FIN + 1) * 16)
                nc.gpsimd.tensor_tensor(x_rows[:, slot], own_share[:], x_rows[:, slot], ALU.add)\
                  .then_inc(base_ready, 1)

            def scale(e):
                slot = e % FIN
                pool.wait_ge(stats_ready, e + 1)
                if e >= FIN:
                    pool.wait_ge(normed, e - FIN + 1)
                if e >= 1:
                    pool.wait_ge(scale_ready, 2 * e)
                nc.gpsimd.tensor_scalar(m2_part[:], halves[:, slot, 2], 4.0 / F, 4.0 * EPS, ALU.mult, ALU.add)\
                  .then_inc(pool_step, 1)
                nc.gpsimd.tensor_tensor(diff_sq[:], halves[:, slot, 1], halves[:, slot, 1], ALU.mult)\
                  .then_inc(pool_step, 1)
                pool.wait_ge(pool_step, 4 * e + 2)
                nc.gpsimd.tensor_tensor(var4[:], m2_part[:], diff_sq[:], ALU.add).then_inc(pool_step, 1)
                pool.wait_ge(pool_step, 4 * e + 3)
                nc.gpsimd.tensor_tensor(half_rstd[:], var4[:], neg_half[:], ALU.pow).then_inc(pool_step, 1)
                pool.wait_ge(pool_step, 4 * e + 4)
                nc.gpsimd.tensor_tensor(shift[:, slot], halves[:, slot, 0], half_rstd[:], ALU.mult)\
                  .then_inc(scale_ready, 1)
                nc.gpsimd.tensor_scalar(rstd[:, slot], half_rstd[:], 2.0, None, ALU.mult).then_inc(scale_ready, 1)

            pool.wait_ge(ds_ready, G)
            for e in range(2):
                prepare(e)
            for e in range(G):
                if e + 2 < G:
                    prepare(e + 2)
                scale(e)

        @block.scalar
        def _(act):
            def load_x(k, slot):
                act.dma_start(x_rows[:, slot], group(x_g, k)).then_inc(x_in[slot], 16)

            for k in range(FIN):
                load_x(k, k)
            act.wait_ge(wt_done, 1)
            nc.scalar.copy(w_t[:], ps_fin[:, 0, 0:F]).then_inc(wt_copied, 1)

            def copy_x(i, q, more):
                act.wait_ge(xt_done, q * U + i + 1)
                if i >= 2:
                    act.wait_ge(sup_done, q * U + (i - 1))
                nc.scalar.copy(flip[:, i % 2], ps_t[:, i % 2]).then_inc(xt_copied, 1)
                if more:
                    load_x(q * U + (i + FIN), i % FIN)

            def part_at(g, c, t):
                return part[:, g % 2, t, bass.ds(c, 1)]

            def sum_share(chunk_in, g, c, first, unused, summed, before, landed):
                def step(t):
                    if t == first:
                        if not isinstance(before, int) or before > 0:
                            act.wait_ge(summed, before)
                        landed()
                    done = nc.scalar.activation(unused[:, t - first], chunk_in[:, t], ACT.Copy,
                                                accum_out=part_at(g, c, t))
                    if t == T - 1:
                        done.then_inc(summed, 1)
                return [lambda t=t: step(t) for t in range(first, T)]

            def sum_ld(g, i, q):
                return sum_share(ring[:, ring_at(ring_row(g), i)], g, q * U + i, V_LD, unused_ld, ld_sum_a,
                                 q * U + (summed_before(g) + i), lambda: ring_landed(act, ring_row(g), i, q))

            def sum_r(g, i, q):
                n0 = r_ringed_before(g)
                return sum_share(r_ring[:, (n0 + i) % RRING], g, q * U + (i + g + 1 + r_kept(g)), V_R, unused_r, r_sum_a,
                                 q * U + (r_shared_before(g) + i), lambda: r_landed(act, n0, i, q))

            def sum_kept(g, d):
                at, landed, value = kept_at(g, d)
                return sum_share(at, g, g + d, V_R, unused_r, r_sum_a, r_shared_before(g) + r_ringed(g) + d - 1,
                                 lambda: act.wait_ge(landed, value))

            each(act, [(0, 0), (1, 0)], lambda i, q: copy_x(i, q, True))
            for step in sum_ld(0, 0, 0):
                step()
            each(act, runs(2, G - FIN), lambda i, q: copy_x(i, q, True))
            for k in range(G - FIN, G):
                copy_x(k, 0, False)

            def stage_hi(g, i, q):
                if i + l_before(g) >= 2:
                    last = (unit_row(g) + i - 1) if i >= 2 else unit_d(g - 1)
                    act.wait_ge(mm_done, (q * U + last) * T)
                if i == 0:
                    act.wait_ge(ds_ready, g)
                nc.scalar.copy(l_hi[:, (l_before(g) + i) % 2],
                               support[:, bass.ds(q * U + i, 1)].rearrange("p a t f -> p (a t) f"))\
                  .then_inc(l_hi_ready, 1)

            def evac(s0, i, q, j):
                act.wait_ge(trans_done, (q * U + (s0 + i)) * T + (j + 1))
                if s0 + i >= 1:
                    act.wait_ge(mm_done, (q * U + (s0 + i - 1)) * T + (j + 1))
                nc.scalar.copy(a_hi[:, j], ps_t[:, j]).then_inc(hi_done, 1)

            def unit(s0, i, q, more=True, steps=()):
                steps = list(steps)
                for n, j in enumerate((2, 3, 0, 1)):
                    if n < 2 or more:
                        evac(s0, i + n // 2, q, j)
                    if n < len(steps) and steps[n]:
                        steps[n]()
                for step in steps[T:]:
                    step()

            def unit_l(g):
                def body(i, q):
                    unit(unit_row(g), i, q, True, [lambda: stage_hi(g, i + 1, q), *sum_ld(g, i + AHEAD, q)])
                return body

            def split_ds(g):
                act.wait_ge(ds_ready, g + 1)
                if g > 0:
                    act.wait_ge(mm_done, unit_row(g) * T)
                nc.scalar.copy(d_hi[:], support[:, g]).then_inc(d_hi_ready, 1)

            def sum_r_or_kept(g, m):
                if m < r_ringed(g):
                    return sum_r(g, m, 0)
                return sum_kept(g, m - r_ringed(g) + 1) if m < r_ringed(g) + r_kept(g) else []

            def run(steps):
                for step in steps:
                    step()

            evac(0, 0, 0, 0)
            evac(0, 0, 0, 1)
            for m in range(R_FIRST):
                run(sum_r(1, m, 0))
            for g in range(G):
                if g > 0 and early(g):
                    for k in range(g):
                        steps = [lambda: stage_hi(g, k + 1, 0)] if k + 1 < g else []
                        if k + AHEAD <= g:
                            steps += sum_ld(g, k + AHEAD, 0)
                        steps += sum_r_or_kept(g, r_with_c(g) + k)
                        if k == g - 1 and total_first(g):
                            steps = [None, None, lambda: split_ds(g)]
                        unit(unit_row(g), k, 0, True, steps)
                    rest_of_r(act, g, lambda i, q: run(sum_r(g, i, q)), lambda d: run(sum_kept(g, d)))
                elif g > 0:
                    each(act, runs(0, g - 1), unit_l(g))
                    unit(unit_row(g), g - 1, 0, True, [None, None, lambda: split_ds(g)])
                if not total_first(g):
                    split_ds(g)
                unit(unit_d(g), 0, 0, True, sum([sum_r_or_kept(g + 1, m) for m in r_in_unit(g, -1)], []))
                act.wait_ge(mm_done, (unit_d(g) + 1) * T)
                nc.scalar.copy(y_acc[:, g] if g < LAST else flip[:, 0], ps_row[:, 0]).then_inc(row_saved, 1)
                if g < LAST:
                    stage_hi(g + 1, 0, 0)
                if early(g + 1):
                    for k in range(g):
                        steps = sum([sum_r_or_kept(g + 1, m) for m in r_in_unit(g, k)], [])
                        for n in ld_with_c(g, k):
                            steps += sum_ld(g + 1, n, 0)
                        unit(unit_c(g), k, 0, True, steps)
                    if g == 0:
                        run(sum_ld(1, 0, 0) + sum_ld(1, 1, 0))
                elif g < LAST:
                    both = r_ringed(g + 1)
                    each(act, [(k, 0) for k in range(min(both, KEEP))] + runs(KEEP, both),
                         lambda i, q: unit(unit_c(g), i, q, True, sum_r(g + 1, i, q)))
                    hidden = g - AHEAD - KEEP
                    each(act, [(k, 0) for k in range(both, min(hidden, KEEP))] + runs(max(both, KEEP), hidden),
                         lambda i, q: unit(unit_c(g), i, q))
                    for n in range(KEEP):
                        steps = sum_kept(g + 1, n + 1) if n < r_kept(g + 1) else []
                        unit(unit_c(g), hidden + n, 0, True, steps)
                    for n in range(AHEAD):
                        unit(unit_c(g), hidden + KEEP + n, 0, True, sum_ld(g + 1, n, 0))

            def load_res(i, q):
                slot = i % FIN
                act.dma_start(x_rows[:, slot], group(x_g, fin_row(i, q))).then_inc(x_in[slot], 16)

            def norm(i, q, more):
                def step(t):
                    if t == 0:
                        act.wait_ge(scale_ready, q * (2 * U) + 2 * i + 2)
                        if i >= 2:
                            act.wait_ge(stored[i % 2], (q * (U // 2) + i // 2) * 16)
                    done = nc.scalar.activation(result[:, i % 2, t], x_rows[:, i % FIN, t], ACT.Identity,
                                                bias=shift[:, i % FIN, t:t + 1], scale=rstd[:, i % FIN, t:t + 1])
                    if t == T - 1:
                        done.then_inc(normed, 1)
                        act.wait_ge(normed, q * U + i + 1)
                        act.dma_start(group(out_g, fin_row(i, q)), result[:, i % 2]).then_inc(stored[i % 2], 16)
                        if more:
                            load_res(i + FIN, q)
                return [lambda t=t: step(t) for t in range(T)]

            for e in range(FIN):
                load_res(e, 0)
            s0 = unit_c(LAST)
            peeled = LAG + 1 + KEEP
            each(act, [(k, 0) for k in range(peeled)] + runs(peeled, LAST - 1),
                 lambda i, q: unit(s0, i, q, True, norm(i - LAG, q, True) if i >= LAG else ()))
            unit(s0, LAST - 1, 0, False, norm(LAST - 1 - LAG, 0, False))
            for e in range(LAST - LAG, G):
                run(norm(e, 0, False))
            for k in range(2):
                act.wait_ge(stored[k], G // 2 * 16)

        @block.vector
        def _(dve):
            def sum_ld(g, i, q):
                ring_landed(dve, ring_row(g), i, q)
                nc.vector.tensor_reduce(part[:, g % 2, 0:V_LD, bass.ds(q * U + i, 1)].rearrange("p t a -> p (t a)"),
                                        ring[:, ring_at(ring_row(g), i), 0:V_LD], AX_X, ALU.add).then_inc(ld_sum_v, 1)

            def sum_r(g):
                def body(i, q):
                    n0 = r_ringed_before(g)
                    r_landed(dve, n0, i, q)
                    share = V_R if g else T
                    nc.vector.tensor_reduce(
                        part[:, g % 2, 0:share, bass.ds(q * U + (i + g + 1 + r_kept(g)), 1)].rearrange("p t a -> p (t a)"),
                        r_ring[:, (n0 + i) % RRING, 0:share], AX_X, ALU.add).then_inc(r_sum_v if g else r0_sum, 1)
                return body

            def sum_kept(g, d):
                at, landed, value = kept_at(g, d)
                dve.wait_ge(landed, value)
                share = V_R if g else T
                nc.vector.tensor_reduce(part[:, g % 2, 0:share, g + d], at[:, 0:share], AX_X, ALU.add)\
                  .then_inc(r_sum_v if g else r0_sum, 1)

            def lo(s0, i, q, j):
                dve.wait_ge(hi_done, (q * U + (s0 + i)) * T + (j + 1))
                nc.vector.tensor_tensor(a_lo[:, j], ps_t[:, j], a_hi[:, j].bitcast(F32), ALU.subtract)\
                  .then_inc(lo_done, 1)

            def unit(s0, i, q, more=True, after_2=None, after_3=None, after_0=None):
                lo(s0, i, q, 2)
                if after_2:
                    after_2()
                lo(s0, i, q, 3)
                if after_3:
                    after_3()
                if more:
                    lo(s0, i + 1, q, 0)
                if after_0:
                    after_0()
                if more:
                    lo(s0, i + 1, q, 1)

            def unit_l(g):
                def body(i, q):
                    unit(unit_row(g), i, q, True, lambda: sum_ld(g, i + AHEAD, q))
                return body

            def total(g):
                dve.wait_ge(ld_sum_v, summed_before(g + 1))
                dve.wait_ge(ld_sum_a, summed_before(g + 1))
                if g == 0:
                    dve.wait_ge(r0_sum, r_ringed(0) + r_kept(0))
                else:
                    dve.wait_ge(r_sum_v, r_shared_before(g + 1))
                    dve.wait_ge(r_sum_a, r_shared_before(g + 1))
                nc.vector.tensor_reduce(row_sum[:, g % 2], part[:, g % 2], AX_X, ALU.add).then_inc(row_summed, 1)
                dve.wait_ge(row_summed, g + 1)
                nc.vector.tensor_scalar(deg[:, g], row_sum[:, g % 2], 1.0, None, ALU.add).then_inc(deg_ready, 1)

            def split_ds(g):
                dve.wait_ge(d_hi_ready, g + 1)
                nc.vector.tensor_tensor(d_lo[:], support[:, g], d_hi[:].bitcast(F32), ALU.subtract)\
                  .then_inc(d_lo_ready, 1)

            def add_c(g):
                def body(i, q):
                    n = l_before(g) + i
                    dve.wait_ge(mm_done, (q * U + (unit_c(g) + i + 1)) * T)
                    rows = y_acc[:, bass.ds(c_row(g, i, q), 1)].rearrange("p a c -> p (a c)")
                    to = rows if g < LAST else flip[:, (i + 1) % 2]
                    nc.vector.tensor_tensor(to, rows, ps_col[:, n % 2], ALU.add).then_inc(col_added, 1)
                return body

            def add_bias(i, q):
                dve.wait_ge(sup_done, q * U + i + 1)
                nc.vector.tensor_tensor(support[:, bass.ds(q * U + i, 1)].rearrange("p a t f -> p (a t) f"),
                                        ps_t[:, 2 + i % 2].rearrange("p (t f) -> p t f", f=F),
                                        bias[:].unsqueeze(1).to_broadcast([P, T, F]), ALU.add)\
                  .then_inc(sup_copied, 1)

            def sum_r_or_kept(g, m):
                if m < r_ringed(g):
                    sum_r(g)(m, 0)
                elif m < r_ringed(g) + r_kept(g):
                    sum_kept(g, m - r_ringed(g) + 1)

            sum_ld(0, 0, 0)
            dve.wait_ge(const_in, 32)
            each(dve, runs(0, r_ringed(0)), lambda i, q: (sum_r(0)(i, q), add_bias(i, q)))
            for k in range(r_ringed(0), G):
                add_bias(k, 0)
            for d in range(1, r_kept(0) + 1):
                sum_kept(0, d)
            lo(0, 0, 0, 0)
            lo(0, 0, 0, 1)
            for g in range(G):
                if g > 0 and early(g):
                    for k in range(g):
                        def sums():
                            if k + AHEAD <= g:
                                sum_ld(g, k + AHEAD, 0)
                            sum_r_or_kept(g, r_with_c(g) + k)
                        if k == g - 1 and total_first(g):
                            total(g)
                            unit(unit_row(g), k, 0, True, after_0=lambda: split_ds(g))
                        else:
                            unit(unit_row(g), k, 0, True, sums)
                    rest_of_r(dve, g, sum_r(g), lambda d: sum_kept(g, d))
                elif g > 0:
                    each(dve, runs(0, g - 1), unit_l(g))
                    total(g)
                    unit(unit_row(g), g - 1, 0, True, after_0=lambda: split_ds(g))
                if not total_first(g):
                    total(g)
                    if g == 0:
                        for m in range(R_FIRST):
                            sum_r(1)(m, 0)
                    split_ds(g)
                unit(unit_d(g), 0, 0, True, lambda: [sum_r_or_kept(g + 1, m) for m in r_in_unit(g, -1)])
                if g > 0:
                    dve.wait_ge(row_saved, g)
                    dve.wait_ge(col_added, l_before(g))
                if early(g + 1):
                    for k in range(g):
                        def sums():
                            for m in r_in_unit(g, k):
                                sum_r_or_kept(g + 1, m)
                            for n in ld_with_c(g, k):
                                sum_ld(g + 1, n, 0)
                        unit(unit_c(g), k, 0, True, sums)
                        add_c(g)(k, 0)
                    if g == 0:
                        for n in range(AHEAD):
                            sum_ld(1, n, 0)
                elif g < LAST:
                    both = r_ringed(g + 1)
                    each(dve, [(k, 0) for k in range(min(both, KEEP))] + runs(KEEP, both),
                         lambda i, q: (unit(unit_c(g), i, q, True, lambda: sum_r(g + 1)(i, q)), add_c(g)(i, q)))
                    hidden = g - AHEAD - KEEP
                    each(dve, [(k, 0) for k in range(both, min(hidden, KEEP))] + runs(max(both, KEEP), hidden),
                         lambda i, q: (unit(unit_c(g), i, q), add_c(g)(i, q)))
                    for n in range(KEEP):
                        unit(unit_c(g), hidden + n, 0, True,
                             (lambda: sum_kept(g + 1, n + 1)) if n < r_kept(g + 1) else None)
                        add_c(g)(hidden + n, 0)
                    for n in range(AHEAD):
                        unit(unit_c(g), hidden + KEEP + n, 0, True, lambda: sum_ld(g + 1, n, 0))
                        add_c(g)(hidden + KEEP + n, 0)

            def make_z(i, q, blocks=range(T)):
                e = q * U + i
                if 0 in blocks:
                    dve.wait_ge(base_ready, e + 1)
                    dve.wait_ge(y_turned, e + 1)
                for t in blocks:
                    d = dinv[:, bass.ds(fin_row(i, q), 1), t]
                    done = nc.vector.scalar_tensor_tensor(x_rows[:, i % FIN, t], ps_fin[:, 0, t * P:(t + 1) * P], d,
                                                          x_rows[:, i % FIN, t], ALU.mult, ALU.add)
                if T - 1 in blocks:
                    done.then_inc(z_ready, 1)

            def stats_z(i, q, blocks=range(T)):
                if 0 in blocks:
                    dve.wait_ge(z_ready, q * U + i + 1)
                for t in blocks:
                    done = nc.vector.bn_stats(stats[:, i % 2, t], x_rows[:, i % FIN, t])
                if T - 1 in blocks:
                    done.then_inc(stats_step, 1)

            def halve(i, q):
                slot = i % FIN
                dve.wait_ge(stats_step, q * U + i + 1)
                mean_e, mean_o = stats[:, i % 2, :, 1], stats[:, i % 2, :, 4]
                nc.vector.scalar_tensor_tensor(halves[:, slot, 0], mean_e, -1.0, mean_o, ALU.mult, ALU.subtract)
                nc.vector.tensor_tensor(halves[:, slot, 1], mean_e, mean_o, ALU.subtract)
                nc.vector.tensor_tensor(halves[:, slot, 2], stats[:, i % 2, :, 2], stats[:, i % 2, :, 5], ALU.add)\
                  .then_inc(stats_ready, 1)

            first, second = range(T // 2), range(T // 2, T)

            def last(i, q):
                unit(unit_c(LAST), i, q, i < LAST - 1,
                     (lambda: stats_z(i - 1, q, first)) if i >= 1 else None,
                     (lambda: stats_z(i - 1, q, second)) if i >= 1 else None,
                     lambda: ([halve(i - 1, q)] if i >= 1 else [], make_z(i, q, first)))
                make_z(i, q, second)
                if i >= 2:
                    dve.wait_ge(y_turned, q * U + i)
                add_c(LAST)(i, q)

            each(dve, [(k, 0) for k in range(KEEP + 1)] + runs(KEEP + 1, LAST - 1) + [(LAST - 1, 0)], last)
            stats_z(LAST - 1, 0)
            halve(LAST - 1, 0)
            make_z(LAST, 0)
            stats_z(LAST, 0)
            halve(LAST, 0)

        @block.tensor
        def _(pe):
            pe.wait_ge(const_in, 32)
            pe.wait_ge(const_set, 2)
            nc.tensor.transpose(ps_fin[:, 0, 0:F], w_rows[:], ident[:]).then_inc(wt_done, 1)

            def turn_x(i, q):
                slot = i % 2
                pe.wait_ge(x_in[i % FIN], (q + (i // FIN + 1)) * 16)
                if i >= 2:
                    pe.wait_ge(xt_copied, q * U + (i - 1))
                for t in range(T):
                    done = nc.tensor.transpose(ps_t[:, slot, t * P:(t + 1) * P], x_rows[:, i % FIN, t], ident[:])
                done.then_inc(xt_done, 1)

            def mul_x(i, q):
                slot = i % 2
                pe.wait_ge(xt_copied, q * U + i + 1)
                if i >= 2:
                    pe.wait_ge(sup_copied, q * U + (i - 1))
                for t in range(T):
                    to = ps_t[:, 2 + slot, t * F:(t + 1) * F]
                    done = nc.tensor.matmul(to, flip[:, slot, t * P:(t + 1) * P], w_t[:], start=True, stop=True)
                done.then_inc(sup_done, 1)

            turn_x(0, 0)
            pe.wait_ge(wt_copied, 1)
            each(pe, [(0, 0)] + [(k, 0) for k in range(1, 3)] + runs(3, G - 1),
                 lambda i, q: (turn_x(i + 1, q), mul_x(i, q)))
            mul_x(G - 1, 0)
            pe.wait_ge(sup_copied, G)

            def from_ring(r0, i, q):
                return ring[:, ring_at(r0, i)], lambda: ring_landed(pe, r0, i, q)

            def c_source(g, i, q):
                if i < c_kept(g) and isinstance(q, int):
                    at, landed, value = kept_at(g - 1 - i, i + 1)
                    return at, lambda: pe.wait_ge(landed, value)
                return from_ring(ring_c(g) - c_kept(g), i, q)

            def turn(source, j):
                at, landed = source
                if j == 0:
                    landed()
                for t in range(T):
                    done = nc.tensor.transpose(ps_t[:, j, t * P:(t + 1) * P], at[:, t, j * P:(j + 1) * P], ident[:])
                done.then_inc(trans_done, 1)

            def mul(s0, i, q, j, w_hi, w_lo, to, start, stop):
                pe.wait_ge(lo_done, (q * U + (s0 + i)) * T + (j + 1))
                nc.tensor.matmul(to, w_hi[:, j], a_hi[:, j], start=start, stop=False)
                nc.tensor.matmul(to, w_hi[:, j], a_lo[:, j], start=False, stop=False)
                nc.tensor.matmul(to, w_lo[:, j], a_hi[:, j], start=False, stop=stop).then_inc(mm_done, 1)

            def unit(s0, i, q, source, following, ready, w_hi, w_lo, to, opens, closes, between=None):
                turn(source, 2)
                ready()
                mul(s0, i, q, 0, w_hi, w_lo, to, opens, False)
                turn(source, 3)
                mul(s0, i, q, 1, w_hi, w_lo, to, False, False)
                if following:
                    turn(following, 0)
                if between:
                    between()
                mul(s0, i, q, 2, w_hi, w_lo, to, False, False)
                if following:
                    turn(following, 1)
                mul(s0, i, q, 3, w_hi, w_lo, to, False, closes)

            def unit_of_l(g):
                def body(i, q):
                    n = l_before(g) + i

                    def ready():
                        pe.wait_ge(l_lo_ready, q * U + (n + 1))
                        if i == 0:
                            pe.wait_ge(row_saved, g)
                    unit(unit_row(g), i, q, from_ring(ring_row(g), i, q), from_ring(ring_row(g), i + 1, q), ready,
                         l_hi[:, n % 2], l_lo[:, n % 2], ps_row[:, 0], i == 0, False)
                return body

            def turn_back(i, q):
                e = q * U + i
                if i == 0:
                    pe.wait_ge(row_saved, G)
                else:
                    pe.wait_ge(col_added, e + l_before(LAST))
                    pe.wait_ge(z_ready, e)
                for t in range(T):
                    done = nc.tensor.transpose(ps_fin[:, 0, t * P:(t + 1) * P],
                                               flip[:, i % 2, t * P:(t + 1) * P], ident[:])
                done.then_inc(y_turned, 1)

            def unit_of_c(g, more=True):
                def body(i, q):
                    n = l_before(g) + i

                    def ready():
                        if n >= 2:
                            pe.wait_ge(col_added, q * U + (n - 1))
                    unit(unit_c(g), i, q, c_source(g, i, q), c_source(g, i + 1, q) if more else None, ready,
                         d_hi, d_lo, ps_col[:, n % 2], True, True, (lambda: turn_back(i, q)) if g == LAST else None)
                return body

            turn(from_ring(0, 0, 0), 0)
            turn(from_ring(0, 0, 0), 1)
            for g in range(G):
                if g > 0:
                    each(pe, [(0, 0)] + runs(1, g), unit_of_l(g))
                unit(unit_d(g), 0, 0, from_ring(ring_row(g), g, 0), c_source(g, 0, 0),
                     lambda: pe.wait_ge(d_lo_ready, g + 1), d_hi, d_lo, ps_row[:, 0], g == 0, True)
                if g < LAST:
                    each(pe, [(k, 0) for k in range(c_kept(g))] + runs(c_kept(g), g), unit_of_c(g))

            each(pe, [(k, 0) for k in range(KEEP)] + runs(KEEP, LAST - 1), unit_of_c(LAST))
            unit_of_c(LAST, False)(LAST - 1, 0)
            turn_back(LAST, 0)


_INS = ['x', 'adj', 'L0_gnn_W', 'L0_gnn_b']


def kernel(**inputs):
    import numpy as _np
    import concourse.bacc as _bacc
    from concourse import mybir as _mybir
    from concourse.bass_utils import run_bass_kernel_spmd as _run

    nc = _bacc.Bacc("TRN2", target_bir_lowering=False, num_devices=1)
    arrays, args = {}, []
    for name in _INS:
        a = _np.ascontiguousarray(inputs[name])
        arrays[f"in_{name}_dram"] = a
        args.append(nc.dram_tensor(f"in_{name}_dram", a.shape, _mybir.dt.from_np(a.dtype), kind="ExternalInput").ap())
    x = arrays["in_x_dram"]
    args.append(nc.dram_tensor("out_0_dram", x.shape, _mybir.dt.from_np(x.dtype), kind="ExternalOutput").ap())
    resnorm_gnn(nc, *args)
    r = _run(nc, [arrays], core_ids=[0])
    return r.results[0]["out_0_dram"]
```
